# Optimizing a Trainium2 kernel written in Bass

```python
import numpy as np
import jax
import jax.numpy as jnp

def _softmax(x, axis=-1):
    return jax.nn.softmax(x, axis=axis)

def _gelu(x):
    return jax.nn.gelu(x, approximate=True)

def _silu(x):
    return jax.nn.silu(x)

def _sigmoid(x):
    return jax.nn.sigmoid(x)

def _layernorm(x, axis=-1, eps=1e-05):
    m = jnp.mean(x, axis=axis, keepdims=True)
    v = jnp.var(x, axis=axis, keepdims=True)
    return (x - m) / jnp.sqrt(v + eps)

def _scatter_add(tgt, idx, src, axis=0):
    return tgt.at[idx].add(src)

def _segment_sum(src, seg, n):
    return jax.ops.segment_sum(src, seg, n)
kernel_name = 'mk_adj_resnorm_d1_adj_r2_e9f370'

def setup_inputs(seed: int=0):
    np.random.seed(seed)
    _w = jnp.asarray

    def _rec_inputs():
        import jax
        import jax.numpy as jnp
        _gk = jax.random.key(seed)
        x = -0.001003 + 1 * jax.random.normal(jax.random.fold_in(_gk, 1), (6144, 128), jnp.float32)
        _a = jax.random.bernoulli(jax.random.fold_in(_gk, 2), 0.000651042, (6144, 6144))
        _a = jnp.logical_or(_a, jnp.swapaxes(_a, -1, -2))
        _a = jnp.logical_or(_a, jnp.eye(6144, dtype=bool))
        adj = _a.astype(jnp.int32)
        return (x, adj)
    x, adj = _rec_inputs()

    def _L0_gnn_setup():
        import jax, jax.numpy as jnp
        import numpy as np
        M = 6144
        N = 6144
        D = 128
        TEMPERATURE = 0.07
        NEG_PAD = jnp.float32(-2 ** 32 + 1)
        key = jax.random.key(seed)
        k1, k2, k3, k4 = jax.random.split(key, 4)
        xx_anchor = jax.random.normal(k1, (M, D), dtype=jnp.float32)
        inp = jax.random.normal(k2, (N, D), dtype=jnp.float32)
        adj = (jax.random.uniform(k3, (M, N)) < 0.002).astype(jnp.int32)
        limit = jnp.sqrt(6.0 / (D + D)).astype(jnp.float32)
        weight = jax.random.uniform(k4, (D, D), minval=-limit, maxval=limit, dtype=jnp.float32)
        return {'xx_anchor': xx_anchor, 'input': inp, 'adj': adj, 'weight': weight}
    _L0_gnn_all = _L0_gnn_setup()
    _L0_gnn_in = {k: v for k, v in _L0_gnn_all.items() if k in ('input', 'weight')}
    del _L0_gnn_all
    return {'x': x, 'adj': adj, 'L0_gnn_input': _L0_gnn_in['input'], 'L0_gnn_weight': _L0_gnn_in['weight']}

def reference(x, adj, L0_gnn_input, L0_gnn_weight):
    import jax
    import jax.numpy as jnp

    def _L0_gnn_ref(xx_anchor, input, adj, weight):
        import jax, jax.numpy as jnp
        import numpy as np
        M = 6144
        N = 6144
        D = 128
        TEMPERATURE = 0.07
        NEG_PAD = jnp.float32(-2 ** 32 + 1)
        anchor_adj = jnp.einsum('md,de,ne->mn', xx_anchor, weight, input)
        scores = jnp.where(adj > 0, anchor_adj, NEG_PAD)
        atten = jax.nn.softmax(scores / TEMPERATURE, axis=1)
        return atten @ input
    x = _layernorm(x + _L0_gnn_ref(x, L0_gnn_input, adj, L0_gnn_weight), axis=-1)
    return x

_drawn_inputs = setup_inputs


def setup_inputs(seed=0):
    import zlib

    import numpy as np

    out = dict(_drawn_inputs(seed))
    spreads = {}
    factors = {}
    for name, (base, spread) in spreads.items():
        noise = np.random.default_rng([zlib.crc32(name.encode()), seed]).standard_normal(out[name].shape)
        drawn = base * np.exp(spread * noise) if base else spread * noise
        out[name] = jnp.asarray(drawn.astype(out[name].dtype))
    for name, factor in factors.items():
        out[name] = (out[name] * factor).astype(out[name].dtype)
    return out
```

```python
from contextlib import ExitStack

import concourse.bass as bass
from concourse import mybir

P = 128
TEMPERATURE = 0.07
EPS = 1e-5
MASKED = -(2.0**100)
TINY = 2.0**-40
PROB_SHIFT = 2.0**14
EXP_BITS = 0x7F800000


class Steps:

    def __init__(self, eng, sem):
        self.eng, self.sem, self.base, self.n = eng, sem, 0, 0

    def done(self, ins):
        ins.then_inc(self.sem, 1)
        self.n += 1
        self.eng.wait_ge(self.sem, self.base + self.n)

    def enter(self, base):
        self.base, self.n = base, 0


def settle(eng, passed):
    eng.sem_inc(passed, 1)


def wait(eng, sem, value):
    if not isinstance(value, int) or value > 0:
        eng.wait_ge(sem, value)


def build(nc, x, adj, inp, weight, out):
    f32, f16, bf16, i32 = mybir.dt.float32, mybir.dt.float16, mybir.dt.bfloat16, mybir.dt.int32
    ALU, ACT, AX = mybir.AluOpType, mybir.ActivationFunctionType, mybir.AxisListType

    M, D = x.shape
    N = inp.shape[0]
    TILES = 4
    QUARTERS = 4
    CH = 512
    BLOCKS = 12
    QCOLS = N // QUARTERS
    CHUNKS = QCOLS // CH
    GROUPS = M // (TILES * P)
    UNITS = GROUPS * QUARTERS
    NB, MB = N // P, M // P
    assert QCOLS == BLOCKS * P and CHUNKS == 3 and TILES * CHUNKS == BLOCKS and D == P
    LAG = 2
    DVE_TILES, POOL_TILES = (0, 2), (1, 3)

    ctx = ExitStack()
    with ctx:
        def sb(name, shape, dt):
            return ctx.enter_context(nc.sbuf_tensor(name, shape, dt))

        def sem(name):
            return ctx.enter_context(nc.semaphore(name))

        kT = [sb(f"kT_{h}", [P, N], f16) for h in ("high", "low")]
        v = [sb(f"v_{h}", [P, NB, D], f16) for h in ("high", "low")]
        qT = [sb(f"qT_{h}", [P, M], f16) for h in ("high", "low")]
        qg = [sb(f"qg_{h}", [P, TILES * P], f16) for h in ("high", "low")]
        scores = sb("scores", [P, 2, TILES, QCOLS], f32)
        adj_sb = sb("adj_sb", [P, TILES, QCOLS], i32)
        mask = sb("mask", [P, TILES, QCOLS], bf16)
        pT = [sb(f"pT_{h}", [P, 3, CH], f16) for h in ("high", "low")]
        oT = sb("oT", [P, TILES * P], f32)
        acc = sb("acc", [P, TILES, D], f32)
        peak = sb("peak", [P, TILES, 2, 1 + CHUNKS], f32)
        nbias = sb("nbias", [P, TILES], f32)
        shrink = sb("shrink", [P, QUARTERS, TILES], f32)
        sums = sb("sums", [P, QUARTERS, TILES, CHUNKS], f32)
        usum = sb("usum", [P, TILES], f32)
        total = sb("total", [P, TILES], f32)
        rtotal = sb("rtotal", [P, TILES], f32)
        x_res = sb("x_res", [P, TILES, D], f32)
        y = sb("y", [P, TILES, D], f32)
        bn = sb("bn", [P, TILES, 6], f32)
        meanvar = sb("meanvar", [P, TILES, 2], f32)
        rstd = sb("rstd", [P, TILES], f32)
        o_sb = sb("o_sb", [P, TILES, D], f32)
        ident = sb("ident", [P, P], f32)
        w_sb = sb("w_sb", [P, D], f32)
        xT = sb("xT", [P, 2, CH], f32)
        mags = sb("mags", [P, P], f32)
        pow2 = sb("pow2", [P, P], f32)
        wide = sb("wide", [P, 4], f32)
        rec = sb("rec", [P, 3], f32)
        k_scale = sb("k_scale", [P, 1], f32)
        q_scale = sb("q_scale", [P, 1], f32)
        e_scale = sb("e_scale", [P, 1], f32)
        ne_scale = sb("ne_scale", [P, 1], f32)
        o_scale = sb("o_scale", [P, 1], f32)
        half = sb("half", [P, 1], f32)

        S = [ctx.enter_context(nc.psum_tensor(f"S{b}", [P, CH], f32)) for b in range(3)]
        T = [ctx.enter_context(nc.psum_tensor(f"T{b}", [P, CH], f32)) for b in range(3)]
        O = [ctx.enter_context(nc.psum_tensor(f"O{b}", [P, CH], f32)) for b in range(2)]

        v_raw = scores[:, 1].rearrange("p t c -> p (t c)").rearrange("p (b d) -> p b d", d=D)
        x_raw = scores[:, 0].rearrange("p t c -> p (t c)").rearrange("p (b d) -> p b d", d=D)

        v_in, x_in, w_in = sem("v_in"), sem("x_in"), sem("w_in")
        zeroed, ident_ready = sem("zeroed"), sem("ident_ready")
        mags_ready, mags_turned, pow2_ready, pow2_spread, scales_ready = (
            sem("mags_ready"), sem("mags_turned"), sem("pow2_ready"), sem("pow2_spread"), sem("scales_ready"))
        turned, high_set, low_set = sem("turned"), sem("high_set"), sem("low_set")
        xT_ready, q_ready = sem("xT_ready"), sem("q_ready")
        qhigh_set, qlow_set = sem("qhigh_set"), sem("qlow_set")
        v_high, v_low = sem("v_high"), sem("v_low")
        adj_in = [sem(f"adj_in{i}") for i in range(TILES)]
        mask_ready = [sem(f"mask_ready{i}") for i in range(TILES)]
        qg_ready = sem("qg_ready")
        s_ready, s_used, peak_ready, bias_ready = sem("s_ready"), sem("s_used"), sem("peak_ready"), sem("bias_ready")
        exp_done, t_ready, high_ready, low_ready = sem("exp_done"), sem("t_ready"), sem("high_ready"), sem("low_ready")
        pv_done, oT_ready, o_back, merged = sem("pv_done"), sem("oT_ready"), sem("o_back"), sem("merged")
        dve_step, pool_step = sem("dve_step"), sem("pool_step")
        dve_passed, pool_passed = sem("dve_passed"), sem("pool_passed")
        shrunk = sem("shrunk")
        xres_in, stats_ready, out_ready, stored = sem("xres_in"), sem("stats_ready"), sem("out_ready"), sem("stored")


        def exists(U):
            return not isinstance(U, int) or 0 <= U < UNITS

        def periods(eng, period, steps=None, per_group=0):
            for U in (-2, -1, 0):
                period(U, U % QUARTERS, U // QUARTERS)
            at = steps.n if steps else 0
            with eng.Fori(0, GROUPS - 1) as g:
                if steps:
                    steps.enter(g * per_group + at)
                for q in range(1, QUARTERS + 1):
                    period(g * QUARTERS + q, q % QUARTERS, g + q // QUARTERS)
                if steps:
                    assert steps.n == per_group, steps.n
            if steps:
                steps.enter((GROUPS - 1) * per_group + at)
            for U in range(UNITS - 3, UNITS + 1):
                period(U, U % QUARTERS, U // QUARTERS)

        block = ctx.enter_context(nc.Block())

        @block.sync
        def _(sp):
            sp.sem_inc(stored, 1)
            sp.dma_start(v_raw, inp.rearrange("(b p) d -> p b d", p=P)).then_inc(v_in, 16)
            sp.dma_start(w_sb[:], weight).then_inc(w_in, 16)
            sp.dma_start(x_raw, x.rearrange("(b p) d -> p b d", p=P)).then_inc(x_in, 16)

            def load_adj(U, q, g, i):
                rows = adj[bass.ds(g * (TILES * P) + i * P, P), q * QCOLS:(q + 1) * QCOLS]
                sp.dma_start(adj_sb[:, i], rows).then_inc(adj_in[i], 16)

            def load_x(g):
                rows = x[bass.ds(g * (TILES * P), TILES * P), :].rearrange("(t p) d -> p t d", p=P)
                sp.dma_start(x_res[:], rows).then_inc(xres_in, 16)

            for i in range(TILES):
                load_adj(0, 0, 0, i)
            load_x(0)

            def period(U, q, g):
                for ahead, i in ((1, 3), (1, 2), (2, 1), (2, 0)):
                    V = U + ahead
                    if exists(V) and exists(V + 1):
                        wait(sp, mask_ready[i], (V + 1) * (CHUNKS if i in DVE_TILES else 1))
                        vq = (q + ahead + 1) % QUARTERS
                        load_adj(V + 1, vq, g + (q + ahead + 1) // QUARTERS, i)
                if q == 0 and exists(U - 1):
                    sp.wait_ge(out_ready, 1 + TILES * g)
                    rows = out[bass.ds((g - 1) * (TILES * P), TILES * P), :].rearrange("(t p) d -> p t d", p=P)
                    sp.dma_start(rows, o_sb[:]).then_inc(stored, 16)
                    if exists(U):
                        load_x(g)

            periods(sp, period)
            sp.wait_ge(stored, 1 + 16 * GROUPS)

        @block.gpsimd
        def _(pool):
            steps = Steps(pool, pool_step)
            pool.sem_inc(out_ready, 1)
            nc.gpsimd.memset(ident[:], 0.0).then_inc(zeroed, 1)
            pool.wait_ge(zeroed, 1)
            nc.gpsimd.affine_select(out=ident[:], in_=ident[:], compare_op=ALU.not_equal, fill=1.0, base=0,
                                    pattern=[[-1, P]], channel_multiplier=1).then_inc(ident_ready, 1)
            steps.done(nc.gpsimd.memset(half[:], -0.5))

            def copy_q(g, i):
                for h in range(2):
                    last = nc.gpsimd.tensor_copy(qg[h][:, i * P:(i + 1) * P], qT[h][:, bass.ds(g * (TILES * P) + i * P, P)])
                last.then_inc(qg_ready, 1)

            def make_mask(V, i):
                pool.wait_ge(adj_in[i], 16 * (V + 1))
                wait(pool, s_used, BLOCKS * (V - 1) + CHUNKS * (i + 1))
                settle(pool, pool_passed)
                nc.gpsimd.tensor_scalar(mask[:, i], adj_sb[:, i], 0.0, MASKED, ALU.is_le, ALU.mult).then_inc(mask_ready[i], 1)

            def period(U, q, g):
                if q == 3 and exists(U + 1) and exists(U):
                    pool.wait_ge(s_ready, BLOCKS * (U + 1))
                    copy_q(g + 1, 3)
                if exists(U + 1):
                    make_mask(U + 1, 3)
                if exists(U + 2):
                    make_mask(U + 2, 1)
                if q == 2 and exists(U) and exists(U + 2):
                    for i in range(3):
                        pool.wait_ge(s_ready, BLOCKS * (U + 1) + CHUNKS * (i + 1))
                        copy_q(g + 1, i)
                if isinstance(U, int) and U == -2:
                    pool.wait_ge(qhigh_set, M // CH)
                    pool.wait_ge(qlow_set, M // CH)
                    for i in range(TILES):
                        copy_q(0, i)
                if q == 0 and exists(U - 1):
                    for t in range(TILES):
                        pool.wait_ge(stats_ready, TILES * (g - 1) + t + 1)
                        if t == 0:
                            wait(pool, stored, 1 + 16 * (g - 1))
                        settle(pool, pool_passed)
                        r = rstd[:, t:t + 1]
                        steps.done(nc.gpsimd.tensor_scalar(r, meanvar[:, t, 1:2], 1.0, EPS, ALU.mult, ALU.add))
                        steps.done(nc.gpsimd.tensor_tensor(r, r, half[:], ALU.pow))
                        settle(pool, pool_passed)
                        nc.gpsimd.tensor_scalar(o_sb[:, t], y[:, t], meanvar[:, t, 0:1], r,
                                                ALU.subtract, ALU.mult).then_inc(out_ready, 1)

            periods(pool, period, steps, 2 * TILES)

        @block.tensor
        def _(pe):
            def product_of_x(b):
                pe.wait_ge(xT_ready, b + 1)
                if b >= 2:
                    pe.wait_ge(qlow_set, b - 1)
                nc.tensor.matmul(S[b % 2][:], w_sb[:], xT[:, b % 2], start=True, stop=True).then_inc(q_ready, 1)

            pe.sem_inc(o_back, 1)
            pe.wait_ge(ident_ready, 1)
            pe.wait_ge(mags_ready, 1)
            nc.tensor.transpose(S[0][:, 0:P], mags[:], ident[:]).then_inc(mags_turned, 1)
            pe.wait_ge(pow2_ready, 1)
            nc.tensor.matmul(S[1][:, 0:4], pow2[:], ident[:, 0:4], start=True, stop=True).then_inc(pow2_spread, 1)
            for b in range(2 * (N // CH)):
                if b == 0:
                    pe.wait_ge(v_in, 16)
                if b >= N // CH + 3:
                    pe.wait_ge(xT_ready, b - 2 - N // CH)
                elif b >= 3:
                    pe.wait_ge(low_set, b - 2)
                if b == N // CH:
                    pe.wait_ge(x_in, 16)
                    pe.wait_ge(w_in, 16)
                raw = v_raw if b < N // CH else x_raw
                for j in range(CH // P):
                    last = nc.tensor.transpose(T[b % 3][:, j * P:(j + 1) * P], raw[:, (b * CH // P + j) % NB, :], ident[:])
                last.then_inc(turned, 1)
                if b > N // CH:
                    product_of_x(b - N // CH - 1)
            product_of_x(N // CH - 1)

            def scores_of(U, q, k):
                V, vq = U + 1, (q + 1) % QUARTERS
                i, c = divmod(k, CHUNKS)
                wait(pe, s_used, BLOCKS * V + k - 2)
                if vq == 0 and c == 0:
                    pe.wait_ge(qg_ready, V + i + 1)
                cols = slice(vq * QCOLS + c * CH, vq * QCOLS + (c + 1) * CH)
                rows = slice(i * P, (i + 1) * P)
                bank = S[k % 3]
                nc.tensor.matmul(bank[:], qg[0][:, rows], kT[0][:, cols], start=True, stop=False)
                nc.tensor.matmul(bank[:], qg[0][:, rows], kT[1][:, cols], start=False, stop=False)
                nc.tensor.matmul(bank[:], qg[1][:, rows], kT[0][:, cols], start=False, stop=True).then_inc(s_ready, 1)

            def turn(U, q, k):
                c = k // 4
                if k % 4 == 0:
                    pe.wait_ge(exp_done, BLOCKS * U + CHUNKS * (TILES - 1) + c + 1)
                wait(pe, low_ready, BLOCKS * U + k - 2)
                for i in range(TILES):
                    last = nc.tensor.transpose(T[k % 3][:, i * P:(i + 1) * P], scores[:, q % 2, i, k * P:(k + 1) * P], ident[:])
                last.then_inc(t_ready, 1)

            def product(U, q, j):
                pe.wait_ge(low_ready, BLOCKS * U + j + 1)
                if j == 0:
                    wait(pe, merged, 1 + TILES * (U - 1))
                    if isinstance(U, int) and U == 0:
                        pe.wait_ge(v_high, 1)
                        pe.wait_ge(v_low, 1)
                n = q * BLOCKS + j
                a = dict(start=(j == 0), stop=False)
                nc.tensor.matmul(O[q % 2][:], v[0][:, n, :], pT[0][:, j % 3], **a)
                nc.tensor.matmul(O[q % 2][:], v[0][:, n, :], pT[1][:, j % 3], start=False, stop=False)
                nc.tensor.matmul(O[q % 2][:], v[1][:, n, :], pT[0][:, j % 3], start=False,
                                 stop=(j == BLOCKS - 1)).then_inc(pv_done, 1)

            def turn_back(U, q):
                pe.wait_ge(oT_ready, U + 1)
                for i in range(TILES):
                    last = nc.tensor.transpose(O[q % 2][:, i * P:(i + 1) * P], oT[:, i * P:(i + 1) * P], ident[:])
                last.then_inc(o_back, 1)

            def period(U, q, g):
                for k in range(BLOCKS):
                    if exists(U + 1):
                        scores_of(U, q, k)
                    if k == 0:
                        if exists(U - 1):
                            product(U - 1, (q - 1) % QUARTERS, BLOCKS - LAG)
                        if exists(U):
                            turn(U, q, k)
                        continue
                    if exists(U):
                        turn(U, q, k)
                    if k >= LAG:
                        if exists(U):
                            product(U, q, k - LAG)
                    elif exists(U - 1):
                        product(U - 1, (q - 1) % QUARTERS, BLOCKS + k - LAG)
                    if k == 3 and exists(U - 1):
                        turn_back(U - 1, (q - 1) % QUARTERS)

            periods(pe, period)

        @block.scalar
        def _(act):
            act.wait_ge(scales_ready, 1)
            for b in range(N // CH):
                act.wait_ge(turned, b + 1)
                nc.scalar.activation(kT[0][:, b * CH:(b + 1) * CH], T[b % 3][:], ACT.Copy, scale=k_scale[:]).then_inc(high_set, 1)
            for b in range(M // CH + 1):
                if b < M // CH:
                    act.wait_ge(turned, N // CH + b + 1)
                    if b >= 2:
                        act.wait_ge(q_ready, b - 1)
                    nc.scalar.copy(xT[:, b % 2], T[b % 3][:]).then_inc(xT_ready, 1)
                if b >= 1:
                    act.wait_ge(q_ready, b)
                    nc.scalar.activation(qT[0][:, (b - 1) * CH:b * CH], S[(b - 1) % 2][:], ACT.Copy,
                                         scale=q_scale[:]).then_inc(qhigh_set, 1)
            nc.scalar.activation(v[0][:], v_raw, ACT.Copy, scale=k_scale[:]).then_inc(v_high, 1)

            def exponentials(V, vq, i, c):
                if c == 0:
                    act.wait_ge(bias_ready, TILES * V + i + 1)
                    if vq:
                        nc.scalar.activation(shrink[:, vq, i:i + 1], peak[:, i, vq % 2, 0:1], ACT.Exp,
                                             bias=nbias[:, i:i + 1], scale=e_scale[:]).then_inc(shrunk, 1)
                p = scores[:, vq % 2, i, c * CH:(c + 1) * CH]
                nc.scalar.activation(p, p, ACT.Exp, bias=nbias[:, i:i + 1], scale=e_scale[:],
                                     accum_out=sums[:, vq, i, c:c + 1]).then_inc(exp_done, 1)

            def split_high(U, q, k):
                act.wait_ge(t_ready, BLOCKS * U + k + 1)
                wait(act, pv_done, BLOCKS * U + k - 2)
                nc.scalar.activation(pT[0][:, k % 3], T[k % 3][:], ACT.Copy, scale=PROB_SHIFT).then_inc(high_ready, 1)

            def period(U, q, g):
                for k in range(BLOCKS):
                    if k < CHUNKS:
                        if exists(U):
                            exponentials(U, q, TILES - 1, k)
                    elif exists(U + 1):
                        exponentials(U + 1, (q + 1) % QUARTERS, k // CHUNKS - 1, k % CHUNKS)
                    if exists(U):
                        split_high(U, q, k)
                    if k == 2 and exists(U - 1):
                        act.wait_ge(pv_done, BLOCKS * U)
                        wait(act, o_back, 1 + U - 1)
                        nc.scalar.copy(oT[:], O[(q - 1) % 2][:]).then_inc(oT_ready, 1)

            periods(act, period)

        @block.vector
        def _(dve):
            steps = Steps(dve, dve_step)
            dve.sem_inc(merged, 1)
            steps.done(nc.vector.memset(mags[:], 0.0))
            dve.wait_ge(w_in, 16)
            nc.vector.tensor_reduce(mags[:, 2:3], w_sb[:], AX.X, ALU.max, apply_absolute_value=True)
            dve.wait_ge(v_in, 16)
            nc.vector.tensor_reduce(mags[:, 0:1], v_raw, AX.XY, ALU.max, apply_absolute_value=True)
            dve.wait_ge(x_in, 16)
            nc.vector.tensor_reduce(mags[:, 1:2], x_raw, AX.XY, ALU.max, apply_absolute_value=True).then_inc(mags_ready, 1)
            dve.wait_ge(mags_turned, 1)
            steps.done(nc.vector.tensor_reduce(pow2[:, 0:1], S[0][:, 0:P], AX.X, ALU.max))
            steps.done(nc.vector.tensor_scalar(pow2[:, 0:1], pow2[:, 0:1], TINY, None, ALU.max))
            steps.done(nc.vector.tensor_scalar(pow2[:, 1:2].bitcast(i32), pow2[:, 0:1].bitcast(i32), EXP_BITS, None,
                                               ALU.bitwise_and))
            nc.vector.tensor_copy(pow2[:, 2:P], pow2[:, 1:2].to_broadcast([P, P - 2]))
            nc.vector.tensor_copy(pow2[:, 0:1], pow2[:, 1:2]).then_inc(pow2_ready, 1)
            dve.wait_ge(pow2_spread, 1)
            steps.done(nc.vector.tensor_copy(wide[:], S[1][:, 0:4]))
            steps.done(nc.vector.tensor_scalar(rec[:].bitcast(i32), wide[:, 0:3].bitcast(i32), -1.0, float(254 << 23),
                                               ALU.mult, ALU.add))
            nc.vector.tensor_scalar(k_scale[:], rec[:, 0:1], 2.0**14, None, ALU.mult)
            nc.vector.tensor_scalar(q_scale[:], rec[:, 1:2], rec[:, 2:3], 2.0**6, ALU.mult, ALU.mult)
            nc.vector.tensor_scalar(o_scale[:], wide[:, 0:1], 2.0**-14 / PROB_SHIFT, None, ALU.mult)
            steps.done(nc.vector.tensor_scalar(e_scale[:], wide[:, 0:1], wide[:, 1:2], 2.0**-20 / TEMPERATURE,
                                               ALU.mult, ALU.mult))
            steps.done(nc.vector.tensor_tensor(e_scale[:], e_scale[:], wide[:, 2:3], ALU.mult))
            nc.vector.tensor_scalar(ne_scale[:], e_scale[:], -1.0, None, ALU.mult).then_inc(scales_ready, 1)
            dve.wait_ge(scales_ready, 1)
            for b in range(N // CH):
                dve.wait_ge(high_set, b + 1)
                cols = slice(b * CH, (b + 1) * CH)
                nc.vector.scalar_tensor_tensor(out=kT[1][:, cols], in0=T[b % 3][:], scalar=k_scale[:], in1=kT[0][:, cols],
                                               op0=ALU.mult, op1=ALU.subtract).then_inc(low_set, 1)
            for b in range(M // CH):
                dve.wait_ge(qhigh_set, b + 1)
                cols = slice(b * CH, (b + 1) * CH)
                nc.vector.scalar_tensor_tensor(out=qT[1][:, cols], in0=S[b % 2][:], scalar=q_scale[:], in1=qT[0][:, cols],
                                               op0=ALU.mult, op1=ALU.subtract).then_inc(qlow_set, 1)
            dve.wait_ge(v_high, 1)
            nc.vector.scalar_tensor_tensor(out=v[1][:], in0=v_raw, scalar=k_scale[:], in1=v[0][:],
                                           op0=ALU.mult, op1=ALU.subtract).then_inc(v_low, 1)
            dve.wait_ge(v_low, 1)

            def make_mask(V, i, c):
                if c == 0:
                    dve.wait_ge(adj_in[i], 16 * (V + 1))
                    wait(dve, s_used, BLOCKS * (V - 1) + CHUNKS * (i + 1))
                cols = slice(c * CH, (c + 1) * CH)
                nc.vector.tensor_scalar(mask[:, i, cols], adj_sb[:, i, cols], 0.0, MASKED,
                                        ALU.is_le, ALU.mult).then_inc(mask_ready[i], 1)

            def add_mask(V, vq, k):
                i, c = divmod(k, CHUNKS)
                dve.wait_ge(s_ready, BLOCKS * V + k + 1)
                if i in DVE_TILES:
                    dve.wait_ge(mask_ready[i], CHUNKS * V + c + 1)
                elif c == 0:
                    dve.wait_ge(mask_ready[i], V + 1)
                settle(dve, dve_passed)
                cols = slice(c * CH, (c + 1) * CH)
                nc.vector.tensor_tensor_reduce(out=scores[:, vq % 2, i, cols], in0=S[k % 3][:], in1=mask[:, i, cols],
                                               scale=1.0, scalar=-3e38, op0=ALU.add, op1=ALU.max,
                                               accum_out=peak[:, i, vq % 2, 1 + c:2 + c]).then_inc(s_used, 1)
                if c == CHUNKS - 1:
                    dve.wait_ge(s_used, BLOCKS * V + k + 1)
                    wait(dve, exp_done, BLOCKS * (V - 1) + CHUNKS * (i + 1))
                    first = 1 if vq == 0 else 0
                    top = peak[:, i, (vq + 1) % 2, 0:1]
                    steps.done(nc.vector.tensor_reduce(top, peak[:, i, vq % 2, first:], AX.X, ALU.max))
                    nc.vector.tensor_scalar(nbias[:, i:i + 1], top, ne_scale[:], None, ALU.mult).then_inc(bias_ready, 1)

            def split_low(U, q, k):
                dve.wait_ge(high_ready, BLOCKS * U + k + 1)
                nc.vector.scalar_tensor_tensor(out=pT[1][:, k % 3], in0=T[k % 3][:], scalar=PROB_SHIFT, in1=pT[0][:, k % 3],
                                               op0=ALU.mult, op1=ALU.subtract).then_inc(low_ready, 1)

            def merge(U, q, g, t):
                if t == 0:
                    dve.wait_ge(o_back, 1 + U + 1)
                    wait(dve, merged, 1 + TILES * U)
                part = O[q % 2][:, t * P:(t + 1) * P]
                if q == 0:
                    nc.vector.tensor_copy(acc[:, t], part).then_inc(merged, 1)
                else:
                    nc.vector.scalar_tensor_tensor(out=acc[:, t], in0=acc[:, t], scalar=shrink[:, q, t:t + 1], in1=part,
                                                   op0=ALU.mult, op1=ALU.add).then_inc(merged, 1)

            def row_sums(U, q, k):
                if k == 3:
                    steps.done(nc.vector.tensor_reduce((total if q == 0 else usum)[:], sums[:, q], AX.X, ALU.add))
                if q > 0 and k == 5:
                    steps.done(nc.vector.tensor_tensor(total[:], total[:], shrink[:, q], ALU.mult))
                if q > 0 and k == 7:
                    steps.done(nc.vector.tensor_tensor(total[:], total[:], usum[:], ALU.add))

            def finish(g, t):
                if t == 0:
                    steps.done(nc.vector.reciprocal(rtotal[:], total[:]))
                    steps.done(nc.vector.tensor_scalar(rtotal[:], rtotal[:], o_scale[:], None, ALU.mult))
                    dve.wait_ge(xres_in, 16 * (g + 1))
                    dve.wait_ge(merged, 1 + TILES * QUARTERS * (g + 1))
                    wait(dve, out_ready, 1 + TILES * g)
                steps.done(nc.vector.scalar_tensor_tensor(out=y[:, t], in0=acc[:, t], scalar=rtotal[:, t:t + 1],
                                                          in1=x_res[:, t], op0=ALU.mult, op1=ALU.add))
                steps.done(nc.vector.bn_stats(bn[:, t], y[:, t]))
                settle(dve, dve_passed)
                nc.vector.bn_aggr(meanvar[:, t], bn[:, t]).then_inc(stats_ready, 1)

            def period(U, q, g):
                for k in range(BLOCKS):
                    if exists(U + 1):
                        add_mask(U + 1, (q + 1) % QUARTERS, k)
                    if exists(U):
                        split_low(U, q, k)
                    if 3 <= k < 6 and exists(U + 1):
                        make_mask(U + 1, 2, k - 3)
                    if k >= 9 and exists(U + 2):
                        make_mask(U + 2, 0, k - 9)
                    if exists(U - 1):
                        row_sums(U - 1, (q - 1) % QUARTERS, k)
                        if 4 <= k < 8:
                            merge(U - 1, (q - 1) % QUARTERS, g, k - 4)
                        if k >= 8 and q == 0:
                            finish(g - 1, k - 8)

            per_group = TILES * QUARTERS + 3 * (QUARTERS - 1) + 1 + 2 + 2 * TILES
            periods(dve, period, steps, per_group)


_INS = ["x", "adj", "L0_gnn_input", "L0_gnn_weight"]
_OUTS = [((6144, 128), "float32")]


def kernel(**inputs):
    import numpy as _np
    import concourse.bacc as _bacc
    from concourse import mybir as _mybir
    from concourse.bass_utils import run_bass_kernel_spmd as _run

    nc = _bacc.Bacc("TRN2", target_bir_lowering=False, num_devices=1)
    arrays, args = {}, []
    for name in _INS:
        a = _np.ascontiguousarray(inputs[name])
        arrays[f"in_{name}_dram"] = a
        args.append(nc.dram_tensor(f"in_{name}_dram", a.shape, _mybir.dt.from_np(a.dtype), kind="ExternalInput").ap())
    for i, (shape, dtype) in enumerate(_OUTS):
        dt = _mybir.dt.from_np(_np.dtype(dtype))
        args.append(nc.dram_tensor(f"out_{i}_dram", shape, dt, kind="ExternalOutput").ap())
    build(nc, *args)
    r = _run(nc, [arrays], core_ids=[0])
    return r.results[0]["out_0_dram"]
```

```python
from contextlib import ExitStack

import concourse.bass as bass
from concourse import mybir

P = 128
TEMPERATURE = 0.07
EPS = 1e-5
MASKED = -(2.0**100)
TINY = 2.0**-40
PROB_SHIFT = 2.0**14
EXP_BITS = 0x7F800000


class Steps:

    def __init__(self, eng, sem):
        self.eng, self.sem, self.base, self.n = eng, sem, 0, 0

    def mark(self, ins):
        ins.then_inc(self.sem, 1)
        self.n += 1
        return self.n

    def reach(self, n):
        self.eng.wait_ge(self.sem, self.base + n)

    def done(self, ins):
        self.reach(self.mark(ins))

    def enter(self, base):
        self.base, self.n = base, 0


def settle(eng, passed):
    eng.sem_inc(passed, 1)


def wait(eng, sem, value):
    if not isinstance(value, int) or value > 0:
        eng.wait_ge(sem, value)


def build(nc, x, adj, inp, weight, out):
    f32, f16, bf16, i32 = mybir.dt.float32, mybir.dt.float16, mybir.dt.bfloat16, mybir.dt.int32
    ALU, ACT, AX = mybir.AluOpType, mybir.ActivationFunctionType, mybir.AxisListType

    M, D = x.shape
    N = inp.shape[0]
    TILES = 4
    QUARTERS = 4
    CH = 512
    BLOCKS = 12
    QCOLS = N // QUARTERS
    CHUNKS = QCOLS // CH
    GROUPS = M // (TILES * P)
    UNITS = GROUPS * QUARTERS
    NB, MB = N // P, M // P
    assert QCOLS == BLOCKS * P and CHUNKS == 3 and TILES * CHUNKS == BLOCKS and D == P
    PIECES = 4
    LAG = 2
    LEAD = 1
    DVE_TILES, POOL_TILES = (0, 2), (1, 3)

    ctx = ExitStack()
    with ctx:
        def sb(name, shape, dt):
            return ctx.enter_context(nc.sbuf_tensor(name, shape, dt))

        def sem(name):
            return ctx.enter_context(nc.semaphore(name))

        kT = [sb(f"kT_{h}", [P, N], f16) for h in ("high", "low")]
        v = [sb(f"v_{h}", [P, NB, D], f16) for h in ("high", "low")]
        qT = [sb(f"qT_{h}", [P, M], f16) for h in ("high", "low")]
        qg = [sb(f"qg_{h}", [P, TILES * P], f16) for h in ("high", "low")]
        scores = sb("scores", [P, 2, TILES, QCOLS], f32)
        adj_sb = sb("adj_sb", [P, TILES, QCOLS], i32)
        mask = sb("mask", [P, TILES, QCOLS], bf16)
        pT = [sb(f"pT_{h}", [P, 3, CH], f16) for h in ("high", "low")]
        oT = sb("oT", [P, TILES * P], f32)
        acc = sb("acc", [P, TILES, D], f32)
        peak = sb("peak", [P, TILES, 2, 1 + CHUNKS], f32)
        nbias = sb("nbias", [P, TILES], f32)
        shrink = sb("shrink", [P, QUARTERS, TILES], f32)
        sums = sb("sums", [P, QUARTERS, TILES, CHUNKS], f32)
        usum = sb("usum", [P, TILES], f32)
        total = sb("total", [P, TILES], f32)
        rtotal = sb("rtotal", [P, TILES], f32)
        x_res = sb("x_res", [P, TILES, D], f32)
        y = sb("y", [P, TILES, D], f32)
        bn = sb("bn", [P, TILES, 6], f32)
        meanvar = sb("meanvar", [P, TILES, 2], f32)
        rstd = sb("rstd", [P, TILES], f32)
        o_sb = sb("o_sb", [P, TILES, D], f32)
        ident = sb("ident", [P, P], f32)
        w_sb = sb("w_sb", [P, D], f32)
        xT = sb("xT", [P, 2, CH], f32)
        part_mags = sb("part_mags", [P, PIECES], f32)
        mags = sb("mags", [P, P], f32)
        pow2 = sb("pow2", [P, P], f32)
        wide = sb("wide", [P, 4], f32)
        rec = sb("rec", [P, 3], f32)
        k_scale = sb("k_scale", [P, 1], f32)
        q_scale = sb("q_scale", [P, 1], f32)
        e_scale = sb("e_scale", [P, 1], f32)
        ne_scale = sb("ne_scale", [P, 1], f32)
        o_scale = sb("o_scale", [P, 1], f32)
        half = sb("half", [P, 1], f32)

        S = [ctx.enter_context(nc.psum_tensor(f"S{b}", [P, CH], f32)) for b in range(3)]
        T = [ctx.enter_context(nc.psum_tensor(f"T{b}", [P, CH], f32)) for b in range(3)]
        O = [ctx.enter_context(nc.psum_tensor(f"O{b}", [P, CH], f32)) for b in range(2)]

        v_raw = sb("v_raw", [P, NB, D], f32)
        x_raw = scores[:, 1].rearrange("p t c -> p (t c)").rearrange("p (b d) -> p b d", d=D)
        KB, XB = N // CH, M // CH

        v_in, x_in = [sem(f"v_in{j}") for j in range(PIECES)], [sem(f"x_in{j}") for j in range(PIECES)]
        w_in = sem("w_in")
        zeroed, ident_ready = sem("zeroed"), sem("ident_ready")
        mags_ready, mags_turned, pow2_ready, pow2_spread, scales_ready = (
            sem("mags_ready"), sem("mags_turned"), sem("pow2_ready"), sem("pow2_spread"), sem("scales_ready"))
        turned, high_set, low_set = sem("turned"), sem("high_set"), sem("low_set")
        xT_ready, q_ready = sem("xT_ready"), sem("q_ready")
        qhigh_set, qlow_set = sem("qhigh_set"), sem("qlow_set")
        v_high, v_low = sem("v_high"), sem("v_low")
        adj_in = [sem(f"adj_in{i}") for i in range(TILES)]
        mask_ready = [sem(f"mask_ready{i}") for i in range(TILES)]
        qg_ready = sem("qg_ready")
        s_ready, s_used, peak_ready, bias_ready = sem("s_ready"), sem("s_used"), sem("peak_ready"), sem("bias_ready")
        exp_done, t_ready, high_ready, low_ready = sem("exp_done"), sem("t_ready"), sem("high_ready"), sem("low_ready")
        pv_done, oT_ready, o_back, merged = sem("pv_done"), sem("oT_ready"), sem("o_back"), sem("merged")
        dve_step, pool_step = sem("dve_step"), sem("pool_step")
        dve_passed, pool_passed = sem("dve_passed"), sem("pool_passed")
        shrunk = sem("shrunk")
        xres_in, stats_ready, out_ready, stored = sem("xres_in"), sem("stats_ready"), sem("out_ready"), sem("stored")


        def exists(U):
            return not isinstance(U, int) or 0 <= U < UNITS

        def score_step(U, q, k):
            ahead, k = divmod(k + LEAD, BLOCKS)
            return U + 1 + ahead, (q + 1 + ahead) % QUARTERS, k

        def periods(eng, period, steps=None, per_group=0):
            for U in (-2, -1, 0):
                period(U, U % QUARTERS, U // QUARTERS)
            at = steps.n if steps else 0
            with eng.Fori(0, GROUPS - 1) as g:
                if steps:
                    steps.enter(g * per_group + at)
                for q in range(1, QUARTERS + 1):
                    period(g * QUARTERS + q, q % QUARTERS, g + q // QUARTERS)
                if steps:
                    assert steps.n == per_group, steps.n
            if steps:
                steps.enter((GROUPS - 1) * per_group + at)
            for U in range(UNITS - 3, UNITS + 1):
                period(U, U % QUARTERS, U // QUARTERS)

        block = ctx.enter_context(nc.Block())

        @block.sync
        def _(sp):
            sp.sem_inc(stored, 1)
            for j in range(PIECES):
                part = slice(j * NB // PIECES, (j + 1) * NB // PIECES)
                sp.dma_start(v_raw[:, part], inp.rearrange("(b p) d -> p b d", p=P)[:, part]).then_inc(v_in[j], 16)
            sp.dma_start(w_sb[:], weight).then_inc(w_in, 16)
            for j in range(PIECES):
                part = slice(j * MB // PIECES, (j + 1) * MB // PIECES)
                sp.dma_start(x_raw[:, part], x.rearrange("(b p) d -> p b d", p=P)[:, part]).then_inc(x_in[j], 16)

            def load_adj(U, q, g, i):
                rows = adj[bass.ds(g * (TILES * P) + i * P, P), q * QCOLS:(q + 1) * QCOLS]
                sp.dma_start(adj_sb[:, i], rows).then_inc(adj_in[i], 16)

            def load_x(g):
                rows = x[bass.ds(g * (TILES * P), TILES * P), :].rearrange("(t p) d -> p t d", p=P)
                sp.dma_start(x_res[:], rows).then_inc(xres_in, 16)

            for i in range(TILES):
                load_adj(0, 0, 0, i)
            load_x(0)

            def period(U, q, g):
                for ahead, i in ((1, 3), (1, 2), (2, 1), (2, 0)):
                    V = U + ahead
                    if exists(V) and exists(V + 1):
                        wait(sp, mask_ready[i], (V + 1) * (CHUNKS if i in DVE_TILES else 1))
                        vq = (q + ahead + 1) % QUARTERS
                        load_adj(V + 1, vq, g + (q + ahead + 1) // QUARTERS, i)
                if q == 0 and exists(U - 1):
                    sp.wait_ge(out_ready, 1 + TILES * g)
                    rows = out[bass.ds((g - 1) * (TILES * P), TILES * P), :].rearrange("(t p) d -> p t d", p=P)
                    sp.dma_start(rows, o_sb[:]).then_inc(stored, 16)
                    if exists(U):
                        load_x(g)

            periods(sp, period)
            sp.wait_ge(stored, 1 + 16 * GROUPS)

        @block.gpsimd
        def _(pool):
            steps = Steps(pool, pool_step)
            pool.sem_inc(out_ready, 1)
            nc.gpsimd.memset(ident[:], 0.0).then_inc(zeroed, 1)
            pool.wait_ge(zeroed, 1)
            nc.gpsimd.affine_select(out=ident[:], in_=ident[:], compare_op=ALU.not_equal, fill=1.0, base=0,
                                    pattern=[[-1, P]], channel_multiplier=1).then_inc(ident_ready, 1)
            steps.done(nc.gpsimd.memset(half[:], -0.5))

            def copy_q(g, i):
                for h in range(2):
                    last = nc.gpsimd.tensor_copy(qg[h][:, i * P:(i + 1) * P], qT[h][:, bass.ds(g * (TILES * P) + i * P, P)])
                last.then_inc(qg_ready, 1)

            def make_mask(V, i):
                pool.wait_ge(adj_in[i], 16 * (V + 1))
                wait(pool, s_used, BLOCKS * (V - 1) + CHUNKS * (i + 1))
                settle(pool, pool_passed)
                nc.gpsimd.tensor_scalar(mask[:, i], adj_sb[:, i], 0.0, MASKED, ALU.is_le, ALU.mult).then_inc(mask_ready[i], 1)

            def period(U, q, g):
                if q == 3 and exists(U + 1) and exists(U):
                    pool.wait_ge(s_ready, BLOCKS * (U + 1))
                    copy_q(g + 1, 3)
                if isinstance(U, int) and U == -2:
                    pool.wait_ge(qhigh_set, 1)
                    pool.wait_ge(qlow_set, 1)
                    for i in range(TILES):
                        copy_q(0, i)
                if exists(U + 1):
                    make_mask(U + 1, 3)
                for i in range(3):
                    if i == 2 and exists(U + 2):
                        make_mask(U + 2, 1)
                    if q == 2 and exists(U) and exists(U + 2):
                        pool.wait_ge(s_ready, BLOCKS * (U + 1) + CHUNKS * (i + 1))
                        copy_q(g + 1, i)
                if isinstance(U, int) and U == 0:
                    pool.wait_ge(qlow_set, XB)
                if q == 0 and exists(U - 1):
                    for t in range(TILES):
                        pool.wait_ge(stats_ready, TILES * (g - 1) + t + 1)
                        if t == 0:
                            wait(pool, stored, 1 + 16 * (g - 1))
                        settle(pool, pool_passed)
                        r = rstd[:, t:t + 1]
                        steps.done(nc.gpsimd.tensor_scalar(r, meanvar[:, t, 1:2], 1.0, EPS, ALU.mult, ALU.add))
                        steps.done(nc.gpsimd.tensor_tensor(r, r, half[:], ALU.pow))
                        settle(pool, pool_passed)
                        nc.gpsimd.tensor_scalar(o_sb[:, t], y[:, t], meanvar[:, t, 0:1], r,
                                                ALU.subtract, ALU.mult).then_inc(out_ready, 1)

            periods(pool, period, steps, 2 * TILES)

        @block.tensor
        def _(pe):
            pe.sem_inc(o_back, 1)

            def turn_magnitudes(n):
                pe.wait_ge(ident_ready, 1)
                pe.wait_ge(mags_ready, n)
                nc.tensor.transpose(S[0][:, 0:P], mags[:], ident[:]).then_inc(mags_turned, 1)
                pe.wait_ge(pow2_ready, n)
                nc.tensor.matmul(S[1][:, 0:4], pow2[:], ident[:, 0:4], start=True, stop=True).then_inc(pow2_spread, 1)

            def turn_rows(raw, b, bank):
                for j in range(CH // P):
                    last = nc.tensor.transpose(T[bank][:, j * P:(j + 1) * P], raw[:, b * CH // P + j, :], ident[:])
                last.then_inc(turned, 1)

            def turn_x(b):
                pe.wait_ge(x_in[b * PIECES // XB], 16)
                if b >= 3:
                    pe.wait_ge(xT_ready, b - 2)
                else:
                    pe.wait_ge(low_set, KB - 2 + b)
                turn_rows(x_raw, b, (KB + b) % 3)

            def product_of_x(b):
                pe.wait_ge(xT_ready, b + 1)
                if b == 0:
                    pe.wait_ge(w_in, 16)
                if b >= 2:
                    pe.wait_ge(qlow_set, b - 1)
                nc.tensor.matmul(O[b % 2][:], w_sb[:], xT[:, b % 2], start=True, stop=True).then_inc(q_ready, 1)

            turn_magnitudes(1)
            for b in range(KB):
                if b >= 3:
                    pe.wait_ge(low_set, b - 2)
                turn_rows(v_raw, b, b % 3)
            turn_x(0)
            product_of_x(0)
            turn_magnitudes(2)

            def scores_of(V, vq, k):
                i, c = divmod(k, CHUNKS)
                wait(pe, s_used, BLOCKS * V + k - 2)
                if vq == 0 and c == 0:
                    pe.wait_ge(qg_ready, V + i + 1)
                cols = slice(vq * QCOLS + c * CH, vq * QCOLS + (c + 1) * CH)
                rows = slice(i * P, (i + 1) * P)
                bank = S[k % 3]
                nc.tensor.matmul(bank[:], qg[0][:, rows], kT[0][:, cols], start=True, stop=False)
                nc.tensor.matmul(bank[:], qg[0][:, rows], kT[1][:, cols], start=False, stop=False)
                nc.tensor.matmul(bank[:], qg[1][:, rows], kT[0][:, cols], start=False, stop=True).then_inc(s_ready, 1)

            def turn(U, q, k):
                c = k // 4
                if k % 4 == 0:
                    pe.wait_ge(exp_done, BLOCKS * U + CHUNKS * (TILES - 1) + c + 1)
                wait(pe, low_ready, BLOCKS * U + k - 2)
                for i in range(TILES):
                    last = nc.tensor.transpose(T[k % 3][:, i * P:(i + 1) * P], scores[:, q % 2, i, k * P:(k + 1) * P], ident[:])
                last.then_inc(t_ready, 1)

            def product(U, q, j):
                pe.wait_ge(low_ready, BLOCKS * U + j + 1)
                if j == 0:
                    wait(pe, merged, 1 + TILES * (U - 1))
                    if isinstance(U, int) and U == 0:
                        pe.wait_ge(qlow_set, XB)
                        pe.wait_ge(v_low, CHUNKS)
                n = q * BLOCKS + j
                a = dict(start=(j == 0), stop=False)
                nc.tensor.matmul(O[q % 2][:], v[0][:, n, :], pT[0][:, j % 3], **a)
                nc.tensor.matmul(O[q % 2][:], v[0][:, n, :], pT[1][:, j % 3], start=False, stop=False)
                nc.tensor.matmul(O[q % 2][:], v[1][:, n, :], pT[0][:, j % 3], start=False,
                                 stop=(j == BLOCKS - 1)).then_inc(pv_done, 1)

            def turn_back(U, q):
                pe.wait_ge(oT_ready, U + 1)
                for i in range(TILES):
                    last = nc.tensor.transpose(O[q % 2][:, i * P:(i + 1) * P], oT[:, i * P:(i + 1) * P], ident[:])
                last.then_inc(o_back, 1)

            def period(U, q, g):
                for k in range(BLOCKS):
                    V, vq, vk = score_step(U, q, k)
                    if exists(V):
                        scores_of(V, vq, vk)
                    if isinstance(U, int) and U == -1:
                        if k + 1 < XB:
                            turn_x(k + 1)
                        if k >= 1:
                            product_of_x(k)
                    if k == 0:
                        if exists(U - 1):
                            product(U - 1, (q - 1) % QUARTERS, BLOCKS - LAG)
                        if exists(U):
                            turn(U, q, k)
                        continue
                    if exists(U):
                        turn(U, q, k)
                    if k >= LAG:
                        if exists(U):
                            product(U, q, k - LAG)
                    elif exists(U - 1):
                        product(U - 1, (q - 1) % QUARTERS, BLOCKS + k - LAG)
                    if k == 3 and exists(U - 1):
                        turn_back(U - 1, (q - 1) % QUARTERS)
                if isinstance(U, int) and U == 0:
                    pe.wait_ge(v_low, QUARTERS * CHUNKS)

            periods(pe, period)

        @block.scalar
        def _(act):
            act.wait_ge(scales_ready, 1)
            for b in range(KB):
                act.wait_ge(turned, b + 1)
                nc.scalar.activation(kT[0][:, b * CH:(b + 1) * CH], T[b % 3][:], ACT.Copy, scale=k_scale[:]).then_inc(high_set, 1)

            def copy_xT(b):
                act.wait_ge(turned, KB + b + 1)
                if b >= 2:
                    act.wait_ge(q_ready, b - 1)
                nc.scalar.copy(xT[:, b % 2], T[(KB + b) % 3][:]).then_inc(xT_ready, 1)

            def q_high(b):
                act.wait_ge(q_ready, b + 1)
                nc.scalar.activation(qT[0][:, b * CH:(b + 1) * CH], O[b % 2][:], ACT.Copy, scale=q_scale[:]).then_inc(qhigh_set, 1)

            def v_high_part(j):
                blocks = slice(j * (CH // P), (j + 1) * (CH // P))
                nc.scalar.activation(v[0][:, blocks], v_raw[:, blocks], ACT.Copy, scale=k_scale[:]).then_inc(v_high, 1)

            copy_xT(0)
            act.wait_ge(scales_ready, 2)
            q_high(0)

            def exponentials(V, vq, i, c):
                if c == 0:
                    act.wait_ge(bias_ready, TILES * V + i + 1)
                    if vq:
                        nc.scalar.activation(shrink[:, vq, i:i + 1], peak[:, i, vq % 2, 0:1], ACT.Exp,
                                             bias=nbias[:, i:i + 1], scale=e_scale[:]).then_inc(shrunk, 1)
                p = scores[:, vq % 2, i, c * CH:(c + 1) * CH]
                nc.scalar.activation(p, p, ACT.Exp, bias=nbias[:, i:i + 1], scale=e_scale[:],
                                     accum_out=sums[:, vq, i, c:c + 1]).then_inc(exp_done, 1)

            def split_high(U, q, k):
                act.wait_ge(t_ready, BLOCKS * U + k + 1)
                wait(act, pv_done, BLOCKS * U + k - 2)
                nc.scalar.activation(pT[0][:, k % 3], T[k % 3][:], ACT.Copy, scale=PROB_SHIFT).then_inc(high_ready, 1)

            def period(U, q, g):
                for k in range(BLOCKS):
                    if k < CHUNKS:
                        if exists(U):
                            exponentials(U, q, TILES - 1, k)
                    elif exists(U + 1):
                        exponentials(U + 1, (q + 1) % QUARTERS, k // CHUNKS - 1, k % CHUNKS)
                    if exists(U):
                        split_high(U, q, k)
                    if isinstance(U, int) and U == -1:
                        if k + 1 < XB:
                            copy_xT(k + 1)
                        if k >= 1:
                            q_high(k)
                        if k >= BLOCKS - CHUNKS:
                            v_high_part(k - (BLOCKS - CHUNKS))
                    if isinstance(U, int) and U == 0 and k < NB // (CH // P) - CHUNKS:
                        v_high_part(k + CHUNKS)
                    if k == 2 and exists(U - 1):
                        act.wait_ge(pv_done, BLOCKS * U)
                        wait(act, o_back, 1 + U - 1)
                        nc.scalar.copy(oT[:], O[(q - 1) % 2][:]).then_inc(oT_ready, 1)

            periods(act, period)

        @block.vector
        def _(dve):
            steps = Steps(dve, dve_step)
            dve.sem_inc(merged, 1)
            steps.done(nc.vector.memset(mags[:], 0.0))

            def magnitude(raw, arrived, column, j):
                dve.wait_ge(arrived[j], 16)
                part = slice(j * NB // PIECES, (j + 1) * NB // PIECES)
                n = steps.mark(nc.vector.tensor_reduce(part_mags[:, j:j + 1], raw[:, part], AX.XY, ALU.max,
                                                       apply_absolute_value=True))
                if j == PIECES - 1:
                    steps.reach(n)
                    nc.vector.tensor_reduce(mags[:, column:column + 1], part_mags[:], AX.X, ALU.max).then_inc(mags_ready, 1)

            def powers_of_two(n):
                dve.wait_ge(mags_turned, n)
                steps.done(nc.vector.tensor_reduce(pow2[:, 0:1], S[0][:, 0:P], AX.X, ALU.max))
                steps.done(nc.vector.tensor_scalar(pow2[:, 0:1], pow2[:, 0:1], TINY, None, ALU.max))
                steps.done(nc.vector.tensor_scalar(pow2[:, 1:2].bitcast(i32), pow2[:, 0:1].bitcast(i32), EXP_BITS, None,
                                                   ALU.bitwise_and))
                nc.vector.tensor_copy(pow2[:, 2:P], pow2[:, 1:2].to_broadcast([P, P - 2]))
                nc.vector.tensor_copy(pow2[:, 0:1], pow2[:, 1:2]).then_inc(pow2_ready, 1)
                dve.wait_ge(pow2_spread, n)
                steps.done(nc.vector.tensor_copy(wide[:], S[1][:, 0:4]))
                steps.done(nc.vector.tensor_scalar(rec[:].bitcast(i32), wide[:, 0:3].bitcast(i32), -1.0, float(254 << 23),
                                                   ALU.mult, ALU.add))

            def k_low(b):
                dve.wait_ge(high_set, b + 1)
                cols = slice(b * CH, (b + 1) * CH)
                nc.vector.scalar_tensor_tensor(out=kT[1][:, cols], in0=T[b % 3][:], scalar=k_scale[:], in1=kT[0][:, cols],
                                               op0=ALU.mult, op1=ALU.subtract).then_inc(low_set, 1)

            def q_low(b):
                dve.wait_ge(qhigh_set, b + 1)
                cols = slice(b * CH, (b + 1) * CH)
                nc.vector.scalar_tensor_tensor(out=qT[1][:, cols], in0=O[b % 2][:], scalar=q_scale[:], in1=qT[0][:, cols],
                                               op0=ALU.mult, op1=ALU.subtract).then_inc(qlow_set, 1)

            def v_low_part(j):
                dve.wait_ge(v_high, j + 1)
                blocks = slice(j * (CH // P), (j + 1) * (CH // P))
                nc.vector.scalar_tensor_tensor(out=v[1][:, blocks], in0=v_raw[:, blocks], scalar=k_scale[:],
                                               in1=v[0][:, blocks], op0=ALU.mult, op1=ALU.subtract).then_inc(v_low, 1)

            for j in range(PIECES):
                magnitude(v_raw, v_in, 0, j)
            powers_of_two(1)
            nc.vector.tensor_scalar(k_scale[:], rec[:, 0:1], 2.0**14, None, ALU.mult).then_inc(scales_ready, 1)
            dve.wait_ge(scales_ready, 1)
            dve.wait_ge(w_in, 16)
            nc.vector.tensor_reduce(mags[:, 2:3], w_sb[:], AX.X, ALU.max, apply_absolute_value=True)
            for b in range(KB):
                k_low(b)
                if b % (KB // PIECES) == KB // PIECES - 1:
                    magnitude(x_raw, x_in, 1, b * PIECES // KB)
            powers_of_two(2)
            nc.vector.tensor_scalar(q_scale[:], rec[:, 1:2], rec[:, 2:3], 2.0**6, ALU.mult, ALU.mult)
            nc.vector.tensor_scalar(o_scale[:], wide[:, 0:1], 2.0**-14 / PROB_SHIFT, None, ALU.mult)
            steps.done(nc.vector.tensor_scalar(e_scale[:], wide[:, 0:1], wide[:, 1:2], 2.0**-20 / TEMPERATURE,
                                               ALU.mult, ALU.mult))
            steps.done(nc.vector.tensor_tensor(e_scale[:], e_scale[:], wide[:, 2:3], ALU.mult))
            nc.vector.tensor_scalar(ne_scale[:], e_scale[:], -1.0, None, ALU.mult).then_inc(scales_ready, 1)
            dve.wait_ge(scales_ready, 2)
            q_low(0)

            def make_mask(V, i, c):
                if c == 0:
                    dve.wait_ge(adj_in[i], 16 * (V + 1))
                    wait(dve, s_used, BLOCKS * (V - 1) + CHUNKS * (i + 1))
                cols = slice(c * CH, (c + 1) * CH)
                nc.vector.tensor_scalar(mask[:, i, cols], adj_sb[:, i, cols], 0.0, MASKED,
                                        ALU.is_le, ALU.mult).then_inc(mask_ready[i], 1)

            def add_mask(V, vq, k):
                i, c = divmod(k, CHUNKS)
                dve.wait_ge(s_ready, BLOCKS * V + k + 1)
                if i in DVE_TILES:
                    dve.wait_ge(mask_ready[i], CHUNKS * V + c + 1)
                elif c == 0:
                    dve.wait_ge(mask_ready[i], V + 1)
                settle(dve, dve_passed)
                cols = slice(c * CH, (c + 1) * CH)
                nc.vector.tensor_tensor_reduce(out=scores[:, vq % 2, i, cols], in0=S[k % 3][:], in1=mask[:, i, cols],
                                               scale=1.0, scalar=-3e38, op0=ALU.add, op1=ALU.max,
                                               accum_out=peak[:, i, vq % 2, 1 + c:2 + c]).then_inc(s_used, 1)

            def raise_peak(V, vq, i):
                dve.wait_ge(s_used, BLOCKS * V + CHUNKS * (i + 1))
                first = 1 if vq == 0 else 0
                return steps.mark(nc.vector.tensor_reduce(peak[:, i, (vq + 1) % 2, 0:1], peak[:, i, vq % 2, first:],
                                                          AX.X, ALU.max))

            def set_bias(V, vq, i, raised):
                wait(dve, exp_done, BLOCKS * (V - 1) + CHUNKS * (i + 1))
                steps.reach(raised)
                nc.vector.tensor_scalar(nbias[:, i:i + 1], peak[:, i, (vq + 1) % 2, 0:1], ne_scale[:], None,
                                        ALU.mult).then_inc(bias_ready, 1)

            def split_low(U, q, k):
                dve.wait_ge(high_ready, BLOCKS * U + k + 1)
                nc.vector.scalar_tensor_tensor(out=pT[1][:, k % 3], in0=T[k % 3][:], scalar=PROB_SHIFT, in1=pT[0][:, k % 3],
                                               op0=ALU.mult, op1=ALU.subtract).then_inc(low_ready, 1)

            def merge(U, q, g, t):
                if t == 0:
                    dve.wait_ge(o_back, 1 + U + 1)
                    wait(dve, merged, 1 + TILES * U)
                part = O[q % 2][:, t * P:(t + 1) * P]
                if q == 0:
                    nc.vector.tensor_copy(acc[:, t], part).then_inc(merged, 1)
                else:
                    nc.vector.scalar_tensor_tensor(out=acc[:, t], in0=acc[:, t], scalar=shrink[:, q, t:t + 1], in1=part,
                                                   op0=ALU.mult, op1=ALU.add).then_inc(merged, 1)

            def row_sums(U, q, k):
                if k == 3:
                    marks["sum"] = steps.mark(nc.vector.tensor_reduce((total if q == 0 else usum)[:], sums[:, q], AX.X, ALU.add))
                if q > 0 and k == 4:
                    marks["sum"] = steps.mark(nc.vector.tensor_tensor(total[:], total[:], shrink[:, q], ALU.mult))
                if q > 0 and k == 5:
                    steps.reach(marks["sum"])
                    marks["sum"] = steps.mark(nc.vector.tensor_tensor(total[:], total[:], usum[:], ALU.add))

            def finish(g, k):
                if k == 6:
                    steps.reach(marks["sum"])
                    marks["rtotal"] = steps.mark(nc.vector.reciprocal(rtotal[:], total[:]))
                if k == 7:
                    steps.reach(marks["rtotal"])
                    steps.done(nc.vector.tensor_scalar(rtotal[:], rtotal[:], o_scale[:], None, ALU.mult))
                    dve.wait_ge(xres_in, 16 * (g + 1))
                    wait(dve, out_ready, 1 + TILES * g)
                if 7 <= k < 7 + TILES:
                    t = k - 7
                    dve.wait_ge(merged, 2 + TILES * QUARTERS * (g + 1) - TILES + t)
                    marks["y", t] = steps.mark(nc.vector.scalar_tensor_tensor(
                        out=y[:, t], in0=acc[:, t], scalar=rtotal[:, t:t + 1], in1=x_res[:, t], op0=ALU.mult, op1=ALU.add))
                for t in range(TILES):
                    if k == min(8 + t, BLOCKS - 1):
                        steps.reach(marks["y", t])
                        marks["bn", t] = steps.mark(nc.vector.bn_stats(bn[:, t], y[:, t]))
                    if k == min(9 + t, BLOCKS - 1):
                        steps.reach(marks["bn", t])
                        settle(dve, dve_passed)
                        nc.vector.bn_aggr(meanvar[:, t], bn[:, t]).then_inc(stats_ready, 1)

            marks = {}

            def period(U, q, g):
                setup = U if isinstance(U, int) else None
                for k in range(BLOCKS):
                    V, vq, vk = score_step(U, q, k)
                    if exists(V):
                        if setup == -1 and k == BLOCKS - LEAD:
                            dve.wait_ge(turned, KB + XB)
                        add_mask(V, vq, vk)
                    if exists(U):
                        split_low(U, q, k)
                    if exists(V) and vk % CHUNKS == CHUNKS - 1:
                        raised = raise_peak(V, vq, vk // CHUNKS)
                    if setup == -1 and k >= 1:
                        q_low(k)
                    if 1 <= k < 4 and exists(U + 1):
                        make_mask(U + 1, 2, k - 1)
                    if 8 <= k < 11 and exists(U + 2):
                        make_mask(U + 2, 0, k - 8)
                    if exists(U - 1):
                        if 4 <= k < 8:
                            merge(U - 1, (q - 1) % QUARTERS, g, k - 4)
                    if exists(V) and vk % CHUNKS == CHUNKS - 1:
                        set_bias(V, vq, vk // CHUNKS, raised)
                    if exists(U - 1):
                        row_sums(U - 1, (q - 1) % QUARTERS, k)
                        if q == 0:
                            finish(g - 1, k)
                    if setup == -1 and k >= BLOCKS - CHUNKS:
                        v_low_part(k - (BLOCKS - CHUNKS))
                    if setup == 0 and k < NB // (CH // P) - CHUNKS:
                        v_low_part(k + CHUNKS)

            per_group = TILES * QUARTERS + 3 * (QUARTERS - 1) + 1 + 2 + 2 * TILES
            periods(dve, period, steps, per_group)


_INS = ["x", "adj", "L0_gnn_input", "L0_gnn_weight"]
_OUTS = [((6144, 128), "float32")]


def kernel(**inputs):
    import numpy as _np
    import concourse.bacc as _bacc
    from concourse import mybir as _mybir
    from concourse.bass_utils import run_bass_kernel_spmd as _run

    nc = _bacc.Bacc("TRN2", target_bir_lowering=False, num_devices=1)
    arrays, args = {}, []
    for name in _INS:
        a = _np.ascontiguousarray(inputs[name])
        arrays[f"in_{name}_dram"] = a
        args.append(nc.dram_tensor(f"in_{name}_dram", a.shape, _mybir.dt.from_np(a.dtype), kind="ExternalInput").ap())
    for i, (shape, dtype) in enumerate(_OUTS):
        dt = _mybir.dt.from_np(_np.dtype(dtype))
        args.append(nc.dram_tensor(f"out_{i}_dram", shape, dt, kind="ExternalOutput").ap())
    build(nc, *args)
    r = _run(nc, [arrays], core_ids=[0])
    return r.results[0]["out_0_dram"]
```

```python
from contextlib import ExitStack

import concourse.bass as bass
from concourse import mybir

P = 128
TEMPERATURE = 0.07
EPS = 1e-5
MASKED = -(2.0**100)
TINY = 2.0**-40
PROB_SHIFT = 2.0**14
EXP_BITS = 0x7F800000


class Steps:

    def __init__(self, eng, sem):
        self.eng, self.sem, self.base, self.n = eng, sem, 0, 0

    def mark(self, ins):
        ins.then_inc(self.sem, 1)
        self.n += 1
        return self.n

    def reach(self, n):
        self.eng.wait_ge(self.sem, self.base + n)

    def done(self, ins):
        self.reach(self.mark(ins))

    def enter(self, base):
        self.base, self.n = base, 0


def settle(eng, passed):
    eng.sem_inc(passed, 1)


def wait(eng, sem, value):
    if not isinstance(value, int) or value > 0:
        eng.wait_ge(sem, value)


def build(nc, x, adj, inp, weight, out):
    f32, f16, bf16, i32 = mybir.dt.float32, mybir.dt.float16, mybir.dt.bfloat16, mybir.dt.int32
    ALU, ACT, AX = mybir.AluOpType, mybir.ActivationFunctionType, mybir.AxisListType

    M, D = x.shape
    N = inp.shape[0]
    TILES = 4
    QUARTERS = 4
    CH = 512
    BLOCKS = 12
    QCOLS = N // QUARTERS
    CHUNKS = QCOLS // CH
    GROUPS = M // (TILES * P)
    UNITS = GROUPS * QUARTERS
    NB, MB = N // P, M // P
    assert QCOLS == BLOCKS * P and CHUNKS == 3 and TILES * CHUNKS == BLOCKS and D == P
    K_EDGES, X_EDGES = (0, 12, 24, 36, 44, 48), (0, 12, 24, 36, 48)
    K_PIECES, X_PIECES = len(K_EDGES) - 1, len(X_EDGES) - 1
    assert K_EDGES[-1] == NB and X_EDGES[-1] == MB
    LAG = 2
    FIRST_LOOPED = 2
    LEAD = 2
    DVE_TILES = (0, 2)

    ctx = ExitStack()
    with ctx:
        def sb(name, shape, dt):
            return ctx.enter_context(nc.sbuf_tensor(name, shape, dt))

        def sem(name):
            return ctx.enter_context(nc.semaphore(name))

        kT = [sb(f"kT_{h}", [P, N], f16) for h in ("high", "low")]
        v = [sb(f"v_{h}", [P, NB, D], f16) for h in ("high", "low")]
        qg = [sb(f"qg_{h}", [P, TILES * P], f16) for h in ("high", "low")]
        qT = [sb(f"qT_{h}", [P, M - TILES * P], f16) for h in ("high", "low")]
        scores = sb("scores", [P, 2, TILES, QCOLS], f32)
        adj_sb = sb("adj_sb", [P, TILES, QCOLS], i32)
        mask = sb("mask", [P, TILES, QCOLS], bf16)
        pT = [sb(f"pT_{h}", [P, 3, CH], f16) for h in ("high", "low")]
        oT = sb("oT", [P, TILES * P], f32)
        acc = sb("acc", [P, TILES, D], f32)
        peak = sb("peak", [P, TILES, 2, 1 + CHUNKS], f32)
        nbias = sb("nbias", [P, TILES], f32)
        shrink = sb("shrink", [P, QUARTERS, TILES], f32)
        sums = sb("sums", [P, QUARTERS, TILES, CHUNKS], f32)
        usum = sb("usum", [P, TILES], f32)
        total = sb("total", [P, TILES], f32)
        rtotal = sb("rtotal", [P, TILES], f32)
        x_res = sb("x_res", [P, TILES, D], f32)
        y = sb("y", [P, TILES, D], f32)
        bn = sb("bn", [P, TILES, 6], f32)
        meanvar = sb("meanvar", [P, TILES, 2], f32)
        rstd = sb("rstd", [P, TILES], f32)
        o_sb = sb("o_sb", [P, TILES, D], f32)
        ident = sb("ident", [P, P], f32)
        w_sb = sb("w_sb", [P, D], f32)
        xT = sb("xT", [P, 2, CH], f32)
        part_mags = sb("part_mags", [P, K_PIECES], f32)
        part_squares = sb("part_squares", [P, X_PIECES], f32)
        mags = sb("mags", [P, P], f32)
        pow2 = sb("pow2", [P, P], f32)
        wide = sb("wide", [P, 4], f32)
        rec = sb("rec", [P, 3], f32)
        k_scale = sb("k_scale", [P, 1], f32)
        q_scale = sb("q_scale", [P, 1], f32)
        e_scale = sb("e_scale", [P, 1], f32)
        ne_scale = sb("ne_scale", [P, 1], f32)
        o_scale = sb("o_scale", [P, 1], f32)
        half = sb("half", [P, TILES], f32)

        S = [ctx.enter_context(nc.psum_tensor(f"S{b}", [P, CH], f32)) for b in range(3)]
        T = [ctx.enter_context(nc.psum_tensor(f"T{b}", [P, CH], f32)) for b in range(3)]
        O = [ctx.enter_context(nc.psum_tensor(f"O{b}", [P, CH], f32)) for b in range(2)]

        v_raw = sb("v_raw", [P, NB, D], f32)
        x_raw = scores[:, 1].rearrange("p t c -> p (t c)").rearrange("p (b d) -> p b d", d=D)
        KB, XB = N // CH, M // CH
        FIRST_X = 6
        K_BEFORE_Q = 8
        turns = [("k", b) for b in range(FIRST_X)] + [("x", 0)] + [("k", b) for b in range(FIRST_X, K_BEFORE_Q)]
        BEFORE = len(turns)
        turns_in_step = [[("x", k + 1)] * (k + 1 < XB) + [("k", K_BEFORE_Q + k)] * (K_BEFORE_Q + k < KB)
                         for k in range(BLOCKS)]
        turns += [turn for step in turns_in_step for turn in step]
        assert len(turns) == KB + XB
        V_POOL, V_BEFORE = 4, 6
        v_in_step = {(0, k): V_BEFORE + j for j, k in enumerate((1, 4, 7))}
        v_in_step.update({(1, k): V_BEFORE + 3 + j for j, k in enumerate((1, 4, 7))})
        assert V_BEFORE + len(v_in_step) == KB
        v_low_in_step = {(-1, 1): 2, (-1, 3): 3, (-1, 5): 4, (-1, 7): 5}

        v_in = [sem(f"v_in{j}") for j in range(K_PIECES)]
        x_in = [sem(f"x_in{j}") for j in range(X_PIECES)]
        w_in = sem("w_in")
        squares_ready = sem("squares_ready")
        zeroed, ident_ready = sem("zeroed"), sem("ident_ready")
        mags_ready, mags_turned, pow2_ready, pow2_spread, scales_ready = (
            sem("mags_ready"), sem("mags_turned"), sem("pow2_ready"), sem("pow2_spread"), sem("scales_ready"))
        turned, high_set, low_set = sem("turned"), sem("high_set"), sem("low_set")
        xT_ready, q_ready = sem("xT_ready"), sem("q_ready")
        qhigh_set, qlow_set = sem("qhigh_set"), sem("qlow_set")
        v_high_first, v_high, v_low = sem("v_high_first"), sem("v_high"), sem("v_low")
        adj_in = [sem(f"adj_in{i}") for i in range(TILES)]
        mask_ready = [sem(f"mask_ready{i}") for i in range(TILES)]
        qg_ready = sem("qg_ready")
        s_ready, s_used, bias_ready = sem("s_ready"), sem("s_used"), sem("bias_ready")
        exp_done, t_ready, high_ready, low_ready = sem("exp_done"), sem("t_ready"), sem("high_ready"), sem("low_ready")
        pv_done, oT_ready, o_back, merged = sem("pv_done"), sem("oT_ready"), sem("o_back"), sem("merged")
        dve_step, pool_step = sem("dve_step"), sem("pool_step")
        dve_passed, pool_passed = sem("dve_passed"), sem("pool_passed")
        shrunk, rstd_ready = sem("shrunk"), sem("rstd_ready")
        xres_in, stats_ready, out_ready, stored = sem("xres_in"), sem("stats_ready"), sem("out_ready"), sem("stored")


        def piece_of(b):
            return next(j for j in range(X_PIECES) if b * (CH // P) < X_EDGES[j + 1])

        def q_half(h, b):
            assert CH == TILES * P
            return qg[h][:] if b == 0 else qT[h][:, (b - 1) * CH:b * CH]

        def exists(U):
            return not isinstance(U, int) or 0 <= U < UNITS

        def score_step(U, q, k):
            ahead, k = divmod(k + LEAD, BLOCKS)
            return U + 1 + ahead, (q + 1 + ahead) % QUARTERS, k

        def periods(eng, period, steps=None, per_group=0):
            for U in range(-2, FIRST_LOOPED):
                period(U, U % QUARTERS, U // QUARTERS)
            at = steps.n if steps else 0
            with eng.Fori(0, GROUPS - 1) as g:
                if steps:
                    steps.enter(g * per_group + at)
                for q in range(FIRST_LOOPED, FIRST_LOOPED + QUARTERS):
                    period(g * QUARTERS + q, q % QUARTERS, g + q // QUARTERS)
                if steps:
                    assert steps.n == per_group, steps.n
            if steps:
                steps.enter((GROUPS - 1) * per_group + at)
            for U in range(UNITS - QUARTERS + FIRST_LOOPED, UNITS + 1):
                period(U, U % QUARTERS, U // QUARTERS)

        block = ctx.enter_context(nc.Block())

        @block.sync
        def _(sp):
            sp.sem_inc(stored, 1)
            sp.dma_start(w_sb[:], weight).then_inc(w_in, 16)
            for j in range(K_PIECES):
                part = slice(K_EDGES[j], K_EDGES[j + 1])
                sp.dma_start(v_raw[:, part], inp.rearrange("(b p) d -> p b d", p=P)[:, part]).then_inc(v_in[j], 16)
            for j in range(X_PIECES):
                part = slice(X_EDGES[j], X_EDGES[j + 1])
                sp.dma_start(x_raw[:, part], x.rearrange("(b p) d -> p b d", p=P)[:, part]).then_inc(x_in[j], 16)

            def load_adj(U, q, g, i):
                rows = adj[bass.ds(g * (TILES * P) + i * P, P), q * QCOLS:(q + 1) * QCOLS]
                sp.dma_start(adj_sb[:, i], rows).then_inc(adj_in[i], 16)

            def load_x(g):
                rows = x[bass.ds(g * (TILES * P), TILES * P), :].rearrange("(t p) d -> p t d", p=P)
                sp.dma_start(x_res[:], rows).then_inc(xres_in, 16)

            def store(g):
                sp.wait_ge(out_ready, 1 + TILES * (g + 1))
                rows = out[bass.ds(g * (TILES * P), TILES * P), :].rearrange("(t p) d -> p t d", p=P)
                sp.dma_start(rows, o_sb[:]).then_inc(stored, 16)

            for i in range(TILES):
                load_adj(0, 0, 0, i)
            load_x(0)

            def period(U, q, g):
                for i in (1, 0, 3, 2):
                    if exists(U + 1) and exists(U + 2):
                        wait(sp, mask_ready[i], (U + 2) * (CHUNKS if i in DVE_TILES else 1))
                        load_adj(U + 2, (q + 2) % QUARTERS, g + (q + 2) // QUARTERS, i)
                    if i == 0 and q == 1 and exists(U - 2):
                        store(g - 1)
                        load_x(g)

            periods(sp, period)
            store(GROUPS - 1)
            sp.wait_ge(stored, 1 + 16 * GROUPS)

        @block.gpsimd
        def _(pool):
            steps = Steps(pool, pool_step)
            pool.sem_inc(out_ready, 1)
            nc.gpsimd.memset(ident[:], 0.0).then_inc(zeroed, 1)
            pool.wait_ge(zeroed, 1)
            nc.gpsimd.affine_select(out=ident[:], in_=ident[:], compare_op=ALU.not_equal, fill=1.0, base=0,
                                    pattern=[[-1, P]], channel_multiplier=1).then_inc(ident_ready, 1)
            steps.done(nc.gpsimd.memset(half[:], -0.5))
            pool.wait_ge(scales_ready, 1)
            settle(pool, pool_passed)
            for j in range(V_POOL):
                blocks = slice(j * (CH // P), (j + 1) * (CH // P))
                nc.gpsimd.tensor_scalar(v[0][:, blocks], v_raw[:, blocks], k_scale[:], None,
                                        ALU.mult).then_inc(v_high_first, 1)

            def copy_q(g, i):
                for h in range(2):
                    cols = bass.ds((g - 1) * (TILES * P) + i * P, P)
                    last = nc.gpsimd.tensor_copy(qg[h][:, i * P:(i + 1) * P], qT[h][:, cols])
                last.then_inc(qg_ready, 1)

            def make_mask(V, i):
                pool.wait_ge(adj_in[i], 16 * (V + 1))
                wait(pool, s_used, BLOCKS * (V - 1) + CHUNKS * (i + 1))
                settle(pool, pool_passed)
                nc.gpsimd.tensor_scalar(mask[:, i], adj_sb[:, i], 0.0, MASKED, ALU.is_le, ALU.mult).then_inc(mask_ready[i], 1)

            def period(U, q, g):
                if q == 3 and exists(U + 1) and exists(U):
                    pool.wait_ge(s_ready, BLOCKS * (U + 1))
                    copy_q(g + 1, 3)
                if exists(U + 1):
                    make_mask(U + 1, 3)
                for i in range(3):
                    if i == 2 and exists(U + 2):
                        make_mask(U + 2, 1)
                    if q == 2 and exists(U) and exists(U + 2):
                        pool.wait_ge(s_ready, BLOCKS * (U + 1) + CHUNKS * (i + 1))
                        copy_q(g + 1, i)
                if isinstance(U, int) and U == 0:
                    pool.wait_ge(qlow_set, XB)
                if q == 0 and exists(U - 1):
                    last = not exists(U)
                    for t in range(0, TILES, TILES if last else 1):
                        n = TILES if last else 1
                        pool.wait_ge(stats_ready, TILES * (g - 1) + t + n)
                        if t == 0:
                            wait(pool, stored, 1 + 16 * (g - 1))
                        settle(pool, pool_passed)
                        r = rstd[:, t:t + n]
                        steps.done(nc.gpsimd.tensor_scalar(r, meanvar[:, t:t + n, 1], 1.0, EPS, ALU.mult, ALU.add))
                        power = nc.gpsimd.tensor_tensor(r, r, half[:, 0:n], ALU.pow)
                        if last:
                            power.then_inc(rstd_ready, 1)
                        else:
                            steps.done(power)
                            settle(pool, pool_passed)
                            nc.gpsimd.tensor_scalar(o_sb[:, t], y[:, t], meanvar[:, t, 0:1], r,
                                                    ALU.subtract, ALU.mult).then_inc(out_ready, 1)

            periods(pool, period, steps, 2 * TILES)

        @block.tensor
        def _(pe):
            pe.sem_inc(o_back, 1)

            def turn_magnitudes(n):
                pe.wait_ge(ident_ready, 1)
                pe.wait_ge(mags_ready, n)
                nc.tensor.transpose(S[0][:, 0:P], mags[:], ident[:]).then_inc(mags_turned, 1)

            def spread_powers(n):
                pe.wait_ge(pow2_ready, n)
                nc.tensor.matmul(S[1][:, 0:4], pow2[:], ident[:, 0:4], start=True, stop=True).then_inc(pow2_spread, 1)

            def turn(kind, b):
                n = turns.index((kind, b))
                if n >= 3:
                    was, at = turns[n - 3]
                    pe.wait_ge(low_set if was == "k" else xT_ready, at + 1)
                if kind == "x":
                    pe.wait_ge(x_in[piece_of(b)], 16)
                raw = v_raw if kind == "k" else x_raw
                for j in range(CH // P):
                    last = nc.tensor.transpose(T[n % 3][:, j * P:(j + 1) * P], raw[:, b * CH // P + j, :], ident[:])
                last.then_inc(turned, 1)

            def product_of_x(b):
                pe.wait_ge(xT_ready, b + 1)
                if b == 0:
                    pe.wait_ge(w_in, 16)
                if b >= 2:
                    pe.wait_ge(qlow_set, b - 1)
                nc.tensor.matmul(O[b % 2][:], w_sb[:], xT[:, b % 2], start=True, stop=True).then_inc(q_ready, 1)

            turn_magnitudes(1)
            spread_powers(1)
            for n, (kind, b) in enumerate(turns[:BEFORE]):
                if n == FIRST_X + 1:
                    turn_magnitudes(2)
                turn(kind, b)
            spread_powers(2)
            product_of_x(0)

            def scores_of(V, vq, k):
                i, c = divmod(k, CHUNKS)
                wait(pe, s_used, BLOCKS * V + k - 2)
                if vq == 0 and c == 0:
                    if isinstance(V, int) and V == 0:
                        pe.wait_ge(qlow_set, 1)
                    else:
                        pe.wait_ge(qg_ready, V - TILES + i + 1)
                cols = slice(vq * QCOLS + c * CH, vq * QCOLS + (c + 1) * CH)
                rows = slice(i * P, (i + 1) * P)
                bank = S[k % 3]
                nc.tensor.matmul(bank[:], qg[0][:, rows], kT[0][:, cols], start=True, stop=False)
                nc.tensor.matmul(bank[:], qg[0][:, rows], kT[1][:, cols], start=False, stop=False)
                nc.tensor.matmul(bank[:], qg[1][:, rows], kT[0][:, cols], start=False, stop=True).then_inc(s_ready, 1)

            def turn_block(U, q, k):
                c = k // 4
                if k % 4 == 0:
                    pe.wait_ge(exp_done, BLOCKS * U + CHUNKS * (TILES - 1) + c + 1)
                wait(pe, low_ready, BLOCKS * U + k - 2)
                for i in range(TILES):
                    last = nc.tensor.transpose(T[k % 3][:, i * P:(i + 1) * P], scores[:, q % 2, i, k * P:(k + 1) * P], ident[:])
                last.then_inc(t_ready, 1)

            def product(U, q, j):
                pe.wait_ge(low_ready, BLOCKS * U + j + 1)
                if j == 0:
                    wait(pe, merged, 1 + TILES * (U - 1))
                    if isinstance(U, int) and U == 0:
                        pe.wait_ge(qlow_set, XB)
                        pe.wait_ge(v_low, CHUNKS)
                n = q * BLOCKS + j
                a = dict(start=(j == 0), stop=False)
                nc.tensor.matmul(O[q % 2][:], v[0][:, n, :], pT[0][:, j % 3], **a)
                nc.tensor.matmul(O[q % 2][:], v[0][:, n, :], pT[1][:, j % 3], start=False, stop=False)
                nc.tensor.matmul(O[q % 2][:], v[1][:, n, :], pT[0][:, j % 3], start=False,
                                 stop=(j == BLOCKS - 1)).then_inc(pv_done, 1)

            def turn_back(U, q):
                pe.wait_ge(oT_ready, U + 1)
                for i in range(TILES):
                    last = nc.tensor.transpose(O[q % 2][:, i * P:(i + 1) * P], oT[:, i * P:(i + 1) * P], ident[:])
                last.then_inc(o_back, 1)

            def period(U, q, g):
                for k in range(BLOCKS):
                    V, vq, vk = score_step(U, q, k)
                    if exists(V):
                        scores_of(V, vq, vk)
                    if isinstance(U, int) and U == -1:
                        for kind, b in turns_in_step[k]:
                            turn(kind, b)
                        if k >= 1:
                            product_of_x(k)
                    if k == 0:
                        if exists(U - 1):
                            product(U - 1, (q - 1) % QUARTERS, BLOCKS - LAG)
                        if exists(U):
                            turn_block(U, q, k)
                        continue
                    if exists(U):
                        turn_block(U, q, k)
                    if k >= LAG:
                        if exists(U):
                            product(U, q, k - LAG)
                    elif exists(U - 1):
                        product(U - 1, (q - 1) % QUARTERS, BLOCKS + k - LAG)
                    if k == 3 and exists(U - 1):
                        turn_back(U - 1, (q - 1) % QUARTERS)
                if isinstance(U, int) and U == 1:
                    pe.wait_ge(v_low, QUARTERS * CHUNKS)

            periods(pe, period)

        @block.scalar
        def _(act):
            def squares(j):
                act.wait_ge(x_in[j], 16)
                part = slice(X_EDGES[j], X_EDGES[j + 1])
                scratch = scores[:, 0].rearrange("p t c -> p (t c)").rearrange("p (b d) -> p b d", d=D)
                nc.scalar.activation(scratch[:, part], x_raw[:, part], ACT.Square,
                                     accum_out=part_squares[:, j:j + 1]).then_inc(squares_ready, 1)

            def k_high(b):
                n = turns.index(("k", b))
                act.wait_ge(turned, n + 1)
                nc.scalar.activation(kT[0][:, b * CH:(b + 1) * CH], T[n % 3][:], ACT.Copy, scale=k_scale[:]).then_inc(high_set, 1)

            def copy_xT(b):
                n = turns.index(("x", b))
                act.wait_ge(turned, n + 1)
                if b >= 2:
                    act.wait_ge(q_ready, b - 1)
                nc.scalar.copy(xT[:, b % 2], T[n % 3][:]).then_inc(xT_ready, 1)

            def q_high(b):
                act.wait_ge(q_ready, b + 1)
                nc.scalar.activation(q_half(0, b), O[b % 2][:], ACT.Copy, scale=q_scale[:]).then_inc(qhigh_set, 1)

            def v_high_part(j):
                blocks = slice(j * (CH // P), (j + 1) * (CH // P))
                nc.scalar.activation(v[0][:, blocks], v_raw[:, blocks], ACT.Copy, scale=k_scale[:]).then_inc(v_high, 1)

            squares(0)
            squares(1)
            act.wait_ge(scales_ready, 1)
            for b in range(K_BEFORE_Q):
                if b == FIRST_X:
                    copy_xT(0)
                k_high(b)
                if b in (1, 4):
                    squares(2 + b // 4)
            for j in range(V_POOL, V_BEFORE):
                v_high_part(j)
            act.wait_ge(scales_ready, 2)
            q_high(0)

            def exponentials(V, vq, i, c):
                if c == 0:
                    act.wait_ge(bias_ready, TILES * V + i + 1)
                    if vq:
                        nc.scalar.activation(shrink[:, vq, i:i + 1], peak[:, i, vq % 2, 0:1], ACT.Exp,
                                             bias=nbias[:, i:i + 1], scale=e_scale[:]).then_inc(shrunk, 1)
                p = scores[:, vq % 2, i, c * CH:(c + 1) * CH]
                nc.scalar.activation(p, p, ACT.Exp, bias=nbias[:, i:i + 1], scale=e_scale[:],
                                     accum_out=sums[:, vq, i, c:c + 1]).then_inc(exp_done, 1)

            def split_high(U, q, k):
                act.wait_ge(t_ready, BLOCKS * U + k + 1)
                wait(act, pv_done, BLOCKS * U + k - 2)
                nc.scalar.activation(pT[0][:, k % 3], T[k % 3][:], ACT.Copy, scale=PROB_SHIFT).then_inc(high_ready, 1)

            def period(U, q, g):
                for k in range(BLOCKS):
                    if k < CHUNKS:
                        if exists(U):
                            exponentials(U, q, TILES - 1, k)
                    elif exists(U + 1):
                        exponentials(U + 1, (q + 1) % QUARTERS, k // CHUNKS - 1, k % CHUNKS)
                    if exists(U):
                        split_high(U, q, k)
                    if isinstance(U, int) and U == -1:
                        for kind, b in turns_in_step[k]:
                            (k_high if kind == "k" else copy_xT)(b)
                        if k >= 1:
                            q_high(k)
                    if isinstance(U, int) and (U, k) in v_in_step:
                        v_high_part(v_in_step[U, k])
                    if k == 2 and exists(U - 1):
                        act.wait_ge(pv_done, BLOCKS * U)
                        wait(act, o_back, 1 + U - 1)
                        nc.scalar.copy(oT[:], O[(q - 1) % 2][:]).then_inc(oT_ready, 1)

            periods(act, period)

        @block.vector
        def _(dve):
            steps = Steps(dve, dve_step)
            dve.sem_inc(merged, 1)
            steps.done(nc.vector.memset(mags[:], 0.0))

            def magnitude(j):
                dve.wait_ge(v_in[j], 16)
                part = slice(K_EDGES[j], K_EDGES[j + 1])
                return steps.mark(nc.vector.tensor_reduce(part_mags[:, j:j + 1], v_raw[:, part], AX.XY, ALU.max,
                                                          apply_absolute_value=True))

            def powers_of_two(n, between=()):
                dve.wait_ge(mags_turned, n)
                steps.done(nc.vector.tensor_reduce(pow2[:, 0:1], S[0][:, 0:P], AX.X, ALU.max))
                steps.done(nc.vector.tensor_scalar(pow2[:, 0:1], pow2[:, 0:1], TINY, None, ALU.max))
                steps.done(nc.vector.tensor_scalar(pow2[:, 1:2].bitcast(i32), pow2[:, 0:1].bitcast(i32), EXP_BITS, None,
                                                   ALU.bitwise_and))
                nc.vector.tensor_copy(pow2[:, 2:P], pow2[:, 1:2].to_broadcast([P, P - 2]))
                nc.vector.tensor_copy(pow2[:, 0:1], pow2[:, 1:2]).then_inc(pow2_ready, 1)
                for b in between:
                    k_low(b)
                dve.wait_ge(pow2_spread, n)
                steps.done(nc.vector.tensor_copy(wide[:], S[1][:, 0:4]))
                root = wide[:, 1:2].bitcast(i32)
                steps.done(nc.vector.tensor_scalar(root, root, 0.5, float(127 << 22), ALU.mult, ALU.add))
                steps.done(nc.vector.tensor_scalar(root, root, EXP_BITS, None, ALU.bitwise_and))
                steps.done(nc.vector.tensor_scalar(rec[:].bitcast(i32), wide[:, 0:3].bitcast(i32), -1.0, float(254 << 23),
                                                   ALU.mult, ALU.add))

            def k_low(b):
                dve.wait_ge(high_set, b + 1)
                cols = slice(b * CH, (b + 1) * CH)
                n = turns.index(("k", b))
                nc.vector.scalar_tensor_tensor(out=kT[1][:, cols], in0=T[n % 3][:], scalar=k_scale[:], in1=kT[0][:, cols],
                                               op0=ALU.mult, op1=ALU.subtract).then_inc(low_set, 1)

            def q_low(b):
                dve.wait_ge(qhigh_set, b + 1)
                nc.vector.scalar_tensor_tensor(out=q_half(1, b), in0=O[b % 2][:], scalar=q_scale[:], in1=q_half(0, b),
                                               op0=ALU.mult, op1=ALU.subtract).then_inc(qlow_set, 1)

            def v_low_part(j):
                if j < V_POOL:
                    dve.wait_ge(v_high_first, j + 1)
                else:
                    dve.wait_ge(v_high, j - V_POOL + 1)
                blocks = slice(j * (CH // P), (j + 1) * (CH // P))
                nc.vector.scalar_tensor_tensor(out=v[1][:, blocks], in0=v_raw[:, blocks], scalar=k_scale[:],
                                               in1=v[0][:, blocks], op0=ALU.mult, op1=ALU.subtract).then_inc(v_low, 1)

            dve.wait_ge(w_in, 16)
            nc.vector.tensor_reduce(mags[:, 2:3], w_sb[:], AX.X, ALU.max, apply_absolute_value=True)
            for j in range(K_PIECES):
                last = magnitude(j)
            steps.reach(last)
            nc.vector.tensor_reduce(mags[:, 0:1], part_mags[:], AX.X, ALU.max).then_inc(mags_ready, 1)
            powers_of_two(1)
            nc.vector.tensor_scalar(k_scale[:], rec[:, 0:1], 2.0**14, None, ALU.mult).then_inc(scales_ready, 1)
            dve.wait_ge(scales_ready, 1)
            for b in range(FIRST_X):
                if b == FIRST_X - 1:
                    dve.wait_ge(squares_ready, X_PIECES)
                    nc.vector.tensor_reduce(mags[:, 1:2], part_squares[:], AX.X, ALU.add).then_inc(mags_ready, 1)
                k_low(b)
                if b in (2, 5):
                    v_low_part(b // 3)
            powers_of_two(2, between=range(FIRST_X, K_BEFORE_Q - 1))
            nc.vector.tensor_scalar(q_scale[:], rec[:, 1:2], rec[:, 2:3], 2.0**6, ALU.mult,
                                    ALU.mult).then_inc(scales_ready, 1)
            nc.vector.tensor_scalar(o_scale[:], wide[:, 0:1], 2.0**-14 / PROB_SHIFT, None, ALU.mult)
            steps.done(nc.vector.tensor_scalar(e_scale[:], wide[:, 0:1], wide[:, 1:2], 2.0**-20 / TEMPERATURE,
                                               ALU.mult, ALU.mult))
            steps.done(nc.vector.tensor_tensor(e_scale[:], e_scale[:], wide[:, 2:3], ALU.mult))
            nc.vector.tensor_scalar(ne_scale[:], e_scale[:], -1.0, None, ALU.mult).then_inc(scales_ready, 1)
            dve.wait_ge(scales_ready, 3)
            q_low(0)
            k_low(K_BEFORE_Q - 1)

            def make_mask(V, i, c):
                if c == 0:
                    dve.wait_ge(adj_in[i], 16 * (V + 1))
                    wait(dve, s_used, BLOCKS * (V - 1) + CHUNKS * (i + 1))
                cols = slice(c * CH, (c + 1) * CH)
                nc.vector.tensor_scalar(mask[:, i, cols], adj_sb[:, i, cols], 0.0, MASKED,
                                        ALU.is_le, ALU.mult).then_inc(mask_ready[i], 1)

            def add_mask(V, vq, k):
                i, c = divmod(k, CHUNKS)
                dve.wait_ge(s_ready, BLOCKS * V + k + 1)
                if i in DVE_TILES:
                    dve.wait_ge(mask_ready[i], CHUNKS * V + c + 1)
                elif c == 0:
                    dve.wait_ge(mask_ready[i], V + 1)
                settle(dve, dve_passed)
                cols = slice(c * CH, (c + 1) * CH)
                nc.vector.tensor_tensor_reduce(out=scores[:, vq % 2, i, cols], in0=S[k % 3][:], in1=mask[:, i, cols],
                                               scale=1.0, scalar=-3e38, op0=ALU.add, op1=ALU.max,
                                               accum_out=peak[:, i, vq % 2, 1 + c:2 + c]).then_inc(s_used, 1)

            def raise_peak(V, vq, i):
                dve.wait_ge(s_used, BLOCKS * V + CHUNKS * (i + 1))
                first = 1 if vq == 0 else 0
                return steps.mark(nc.vector.tensor_reduce(peak[:, i, (vq + 1) % 2, 0:1], peak[:, i, vq % 2, first:],
                                                          AX.X, ALU.max))

            def set_bias(V, vq, i, raised):
                wait(dve, exp_done, BLOCKS * (V - 1) + CHUNKS * (i + 1))
                steps.reach(raised)
                nc.vector.tensor_scalar(nbias[:, i:i + 1], peak[:, i, (vq + 1) % 2, 0:1], ne_scale[:], None,
                                        ALU.mult).then_inc(bias_ready, 1)

            def split_low(U, q, k):
                dve.wait_ge(high_ready, BLOCKS * U + k + 1)
                nc.vector.scalar_tensor_tensor(out=pT[1][:, k % 3], in0=T[k % 3][:], scalar=PROB_SHIFT, in1=pT[0][:, k % 3],
                                               op0=ALU.mult, op1=ALU.subtract).then_inc(low_ready, 1)

            def merge(U, q, g, t):
                if t == 0:
                    dve.wait_ge(o_back, 1 + U + 1)
                    wait(dve, merged, 1 + TILES * U)
                part = O[q % 2][:, t * P:(t + 1) * P]
                if q == 0:
                    nc.vector.tensor_copy(acc[:, t], part).then_inc(merged, 1)
                else:
                    nc.vector.scalar_tensor_tensor(out=acc[:, t], in0=acc[:, t], scalar=shrink[:, q, t:t + 1], in1=part,
                                                   op0=ALU.mult, op1=ALU.add).then_inc(merged, 1)

            def row_sums(U, q, k):
                if k == 3:
                    marks["sum"] = steps.mark(nc.vector.tensor_reduce((total if q == 0 else usum)[:], sums[:, q], AX.X, ALU.add))
                if q > 0 and k == 4:
                    marks["sum"] = steps.mark(nc.vector.tensor_tensor(total[:], total[:], shrink[:, q], ALU.mult))
                if q > 0 and k == 5:
                    steps.reach(marks["sum"])
                    marks["sum"] = steps.mark(nc.vector.tensor_tensor(total[:], total[:], usum[:], ALU.add))

            def finish(g, k):
                if k == 6:
                    steps.reach(marks["sum"])
                    marks["rtotal"] = steps.mark(nc.vector.reciprocal(rtotal[:], total[:]))
                if k == 7:
                    steps.reach(marks["rtotal"])
                    steps.done(nc.vector.tensor_scalar(rtotal[:], rtotal[:], o_scale[:], None, ALU.mult))
                    dve.wait_ge(xres_in, 16 * (g + 1))
                    wait(dve, out_ready, 1 + TILES * g)
                if 7 <= k < 7 + TILES:
                    t = k - 7
                    dve.wait_ge(merged, 2 + TILES * QUARTERS * (g + 1) - TILES + t)
                    marks["y", t] = steps.mark(nc.vector.scalar_tensor_tensor(
                        out=y[:, t], in0=acc[:, t], scalar=rtotal[:, t:t + 1], in1=x_res[:, t], op0=ALU.mult, op1=ALU.add))
                for t in range(TILES):
                    if k == min(8 + t, BLOCKS - 1):
                        steps.reach(marks["y", t])
                        marks["bn", t] = steps.mark(nc.vector.bn_stats(bn[:, t], y[:, t]))
                    if k == min(9 + t, BLOCKS - 1):
                        steps.reach(marks["bn", t])
                        settle(dve, dve_passed)
                        nc.vector.bn_aggr(meanvar[:, t], bn[:, t]).then_inc(stats_ready, 1)

            marks = {}

            def period(U, q, g):
                setup = U if isinstance(U, int) else None
                for k in range(BLOCKS):
                    V, vq, vk = score_step(U, q, k)
                    if exists(V):
                        if setup == -1 and k == BLOCKS - LEAD:
                            dve.wait_ge(turned, KB + XB)
                        add_mask(V, vq, vk)
                    last_tile = exists(V) and vk == BLOCKS - 1
                    if last_tile:
                        set_bias(V, vq, TILES - 1, raise_peak(V, vq, TILES - 1))
                    if exists(U):
                        split_low(U, q, k)
                    if exists(V) and vk % CHUNKS == CHUNKS - 1 and not last_tile:
                        raised = raise_peak(V, vq, vk // CHUNKS)
                    if setup == -1:
                        for kind, b in turns_in_step[k]:
                            if kind == "k":
                                k_low(b)
                        if k >= 1:
                            q_low(k)
                    if 1 <= k < 4 and exists(U + 1):
                        make_mask(U + 1, 2, k - 1)
                    if 4 <= k < 7 and exists(U + 2):
                        make_mask(U + 2, 0, k - 4)
                    if exists(U - 1):
                        if 4 <= k < 8:
                            merge(U - 1, (q - 1) % QUARTERS, g, k - 4)
                    if exists(V) and vk % CHUNKS == CHUNKS - 1 and not last_tile:
                        set_bias(V, vq, vk // CHUNKS, raised)
                    if exists(U - 1):
                        row_sums(U - 1, (q - 1) % QUARTERS, k)
                        if q == 0:
                            finish(g - 1, k)
                    if (setup, k) in v_in_step:
                        v_low_part(v_in_step[setup, k])
                    if (setup, k) in v_low_in_step:
                        v_low_part(v_low_in_step[setup, k])

            per_group = TILES * QUARTERS + 3 * (QUARTERS - 1) + 1 + 2 + 2 * TILES
            periods(dve, period, steps, per_group)
            dve.wait_ge(rstd_ready, 1)
            for t in range(TILES):
                nc.vector.tensor_scalar(o_sb[:, t], y[:, t], meanvar[:, t, 0:1], rstd[:, t:t + 1],
                                        ALU.subtract, ALU.mult).then_inc(out_ready, 1)


_INS = ["x", "adj", "L0_gnn_input", "L0_gnn_weight"]
_OUTS = [((6144, 128), "float32")]


def kernel(**inputs):
    import numpy as _np
    import concourse.bacc as _bacc
    from concourse import mybir as _mybir
    from concourse.bass_utils import run_bass_kernel_spmd as _run

    nc = _bacc.Bacc("TRN2", target_bir_lowering=False, num_devices=1)
    arrays, args = {}, []
    for name in _INS:
        a = _np.ascontiguousarray(inputs[name])
        arrays[f"in_{name}_dram"] = a
        args.append(nc.dram_tensor(f"in_{name}_dram", a.shape, _mybir.dt.from_np(a.dtype), kind="ExternalInput").ap())
    for i, (shape, dtype) in enumerate(_OUTS):
        dt = _mybir.dt.from_np(_np.dtype(dtype))
        args.append(nc.dram_tensor(f"out_{i}_dram", shape, dt, kind="ExternalOutput").ap())
    build(nc, *args)
    r = _run(nc, [arrays], core_ids=[0])
    return r.results[0]["out_0_dram"]
```
